# Optimizing a Trainium2 kernel written in Bass

```python
import numpy as np
import jax
import jax.numpy as jnp

def _softmax(x, axis=-1):
    return jax.nn.softmax(x, axis=axis)

def _gelu(x):
    return jax.nn.gelu(x, approximate=True)

def _silu(x):
    return jax.nn.silu(x)

def _sigmoid(x):
    return jax.nn.sigmoid(x)

def _layernorm(x, axis=-1, eps=1e-05):
    m = jnp.mean(x, axis=axis, keepdims=True)
    v = jnp.var(x, axis=axis, keepdims=True)
    return (x - m) / jnp.sqrt(v + eps)

def _scatter_add(tgt, idx, src, axis=0):
    return tgt.at[idx].add(src)

def _segment_sum(src, seg, n):
    return jax.ops.segment_sum(src, seg, n)
kernel_name = 'mk_audio_tower_d1_tok_audfeat512_r4_5fa105'

def setup_inputs(seed: int=0):
    np.random.seed(seed)
    _w = jnp.asarray

    def _rec_inputs():
        import jax
        import jax.numpy as jnp
        _rk = jax.random.key(seed)
        x = -7.10856e-05 + 0.999911 * jax.random.normal(jax.random.fold_in(_rk, 1), (8, 8192, 128), jnp.float32)
        return x
    x = _rec_inputs()

    def _L0_tok_setup():
        import jax, jax.numpy as jnp
        import numpy as np
        B, S, D = (4, 8192, 128)
        CHUNK = 16
        key = jax.random.key(seed)
        k1, k2 = jax.random.split(key)
        x = jax.random.normal(k1, (B, S, D), dtype=jnp.float32)
        W = jax.random.normal(k2, (D, D), dtype=jnp.float32) / np.sqrt(D)
        b = jnp.zeros((D,), dtype=jnp.float32)
        return {'x': x, 'W': W, 'b': b, 'chunk_size': CHUNK}
    _L0_tok_all = _L0_tok_setup()
    _L0_tok_in = {k: v for k, v in _L0_tok_all.items() if k in ('W', 'b')}
    del _L0_tok_all

    def _L0_attn_setup():
        import jax, jax.numpy as jnp
        import numpy as np
        B, T, D = (4, 1024, 128)
        H = 256
        QK = 128
        G = 64

        def _conv_module(x, ln_g, ln_b, w, b, cw, cb):
            mu = jnp.mean(x, axis=-1, keepdims=True)
            var = jnp.mean(jnp.square(x - mu), axis=-1, keepdims=True)
            xn = (x - mu) * jax.lax.rsqrt(var + 1e-05) * ln_g + ln_b
            h = jax.nn.silu(xn @ w + b)
            hp = jnp.pad(h, ((0, 0), (1, 1), (0, 0)))
            conv = hp[:, :-2] * cw[:, 0] + hp[:, 1:-1] * cw[:, 1] + hp[:, 2:] * cw[:, 2] + cb
            return h + conv

        def _rotary(x):
            b, n, d = x.shape
            inv_freq = 1.0 / 10000.0 ** (jnp.arange(0, d, 2, dtype=jnp.float32) / d)
            freqs = jnp.arange(n, dtype=jnp.float32)[:, None] * inv_freq
            emb = jnp.repeat(freqs, 2, axis=-1)
            cos, sin = (jnp.cos(emb), jnp.sin(emb))
            xp = x.reshape(b, n, d // 2, 2)
            rot = jnp.stack([-xp[..., 1], xp[..., 0]], axis=-1).reshape(b, n, d)
            return x * cos + rot * sin

        def _forward(x, u_ln_g, u_ln_b, u_w, u_b, u_cw, u_cb, v_ln_g, v_ln_b, v_w, v_b, v_cw, v_cb, qk_ln_g, qk_ln_b, qk_w, qk_b, qk_cw, qk_cb, out_ln_g, out_ln_b, out_w, out_b, out_cw, out_cb, gamma, beta):
            seq_len = x.shape[1]
            u = _conv_module(x, u_ln_g, u_ln_b, u_w, u_b, u_cw, u_cb)
            v = _conv_module(x, v_ln_g, v_ln_b, v_w, v_b, v_cw, v_cb)
            z = _conv_module(x, qk_ln_g, qk_ln_b, qk_w, qk_b, qk_cw, qk_cb)
            qk4 = z[..., None, :] * gamma + beta
            quad_q = _rotary(qk4[:, :, 0])
            lin_q = _rotary(qk4[:, :, 1])
            quad_k = _rotary(qk4[:, :, 2])
            lin_k = _rotary(qk4[:, :, 3])
            lin_kv = jnp.einsum('bnd,bne->bde', lin_k, v) / seq_len
            lin_ku = jnp.einsum('bnd,bne->bde', lin_k, u) / seq_len
            lin_out_v = jnp.einsum('bnd,bde->bne', lin_q, lin_kv)
            lin_out_u = jnp.einsum('bnd,bde->bne', lin_q, lin_ku)
            pad = -seq_len % G

            def grp(t):
                if pad:
                    t = jnp.pad(t, ((0, 0), (0, pad), (0, 0)))
                return t.reshape(t.shape[0], -1, G, t.shape[-1])
            qq, qk_, ug, vg = (grp(quad_q), grp(quad_k), grp(u), grp(v))
            sim = jnp.einsum('bnid,bnjd->bnij', qq, qk_) / G
            attn = jnp.square(jax.nn.relu(sim))
            quad_out_v = jnp.einsum('bnij,bnjd->bnid', attn, vg).reshape(x.shape[0], -1, vg.shape[-1])[:, :seq_len]
            quad_out_u = jnp.einsum('bnij,bnjd->bnid', attn, ug).reshape(x.shape[0], -1, ug.shape[-1])[:, :seq_len]
            v_hat = quad_out_v + lin_out_v
            u_hat = quad_out_u + lin_out_u
            o_gate = jax.nn.sigmoid(u * v_hat)
            gated = u_hat * v * o_gate
            return _conv_module(gated, out_ln_g, out_ln_b, out_w, out_b, out_cw, out_cb) + x
        key = jax.random.key(seed)
        ks = jax.random.split(key, 16)

        def p(k, shape, scale=0.02):
            return jax.random.normal(k, shape, jnp.float32) * scale
        inp = {'x': jax.random.normal(ks[0], (B, T, D), jnp.float32)}
        i = 1
        for name, (din, dout) in [('u', (D, H)), ('v', (D, H)), ('qk', (D, QK)), ('out', (H, D))]:
            inp[f'{name}_ln_g'] = jnp.ones((din,), jnp.float32)
            inp[f'{name}_ln_b'] = jnp.zeros((din,), jnp.float32)
            inp[f'{name}_w'] = p(ks[i], (din, dout))
            i += 1
            inp[f'{name}_b'] = jnp.zeros((dout,), jnp.float32)
            inp[f'{name}_cw'] = p(ks[i], (dout, 3))
            i += 1
            inp[f'{name}_cb'] = jnp.zeros((dout,), jnp.float32)
        inp['gamma'] = 1.0 + p(ks[i], (4, QK))
        inp['beta'] = jnp.zeros((4, QK), jnp.float32)
        return inp
    _L0_attn_all = _L0_attn_setup()
    _L0_attn_in = {k: v for k, v in _L0_attn_all.items() if k in ('u_ln_g', 'u_ln_b', 'u_w', 'u_b', 'u_cw', 'u_cb', 'v_ln_g', 'v_ln_b', 'v_w', 'v_b', 'v_cw', 'v_cb', 'qk_ln_g', 'qk_ln_b', 'qk_w', 'qk_b', 'qk_cw', 'qk_cb', 'out_ln_g', 'out_ln_b', 'out_w', 'out_b', 'out_cw', 'out_cb', 'gamma', 'beta')}
    del _L0_attn_all

    def _L0_ffn_setup():
        import jax, jax.numpy as jnp
        import numpy as np
        E = 64
        K = 6
        NS = 2
        D = 128
        F = 128

        def _swiglu_ffn(x, wg, wu, wd):
            return jax.nn.silu(x @ wg) * (x @ wu) @ wd
        key = jax.random.key(seed)
        ks = jax.random.split(key, 8)
        s = 0.02
        return {'hidden_states': jax.random.normal(ks[0], (2, 256, D), dtype=jnp.float32), 'Wr': jax.random.normal(ks[1], (D, E), dtype=jnp.float32) * s, 'sWg': jax.random.normal(ks[2], (NS, D, F), dtype=jnp.float32) * s, 'sWu': jax.random.normal(ks[3], (NS, D, F), dtype=jnp.float32) * s, 'sWd': jax.random.normal(ks[4], (NS, F, D), dtype=jnp.float32) * s, 'Wg': jax.random.normal(ks[5], (E, D, F), dtype=jnp.float32) * s, 'Wu': jax.random.normal(ks[6], (E, D, F), dtype=jnp.float32) * s, 'Wd': jax.random.normal(ks[7], (E, F, D), dtype=jnp.float32) * s}
    _L0_ffn_all = _L0_ffn_setup()
    _L0_ffn_in = {k: v for k, v in _L0_ffn_all.items() if k in ('Wr', 'sWg', 'sWu', 'sWd', 'Wg', 'Wu', 'Wd')}
    del _L0_ffn_all
    return {'x': x, 'L0_tok_W': _L0_tok_in['W'], 'L0_tok_b': _L0_tok_in['b'], 'L0_attn_u_ln_g': _L0_attn_in['u_ln_g'], 'L0_attn_u_ln_b': _L0_attn_in['u_ln_b'], 'L0_attn_u_w': _L0_attn_in['u_w'], 'L0_attn_u_b': _L0_attn_in['u_b'], 'L0_attn_u_cw': _L0_attn_in['u_cw'], 'L0_attn_u_cb': _L0_attn_in['u_cb'], 'L0_attn_v_ln_g': _L0_attn_in['v_ln_g'], 'L0_attn_v_ln_b': _L0_attn_in['v_ln_b'], 'L0_attn_v_w': _L0_attn_in['v_w'], 'L0_attn_v_b': _L0_attn_in['v_b'], 'L0_attn_v_cw': _L0_attn_in['v_cw'], 'L0_attn_v_cb': _L0_attn_in['v_cb'], 'L0_attn_qk_ln_g': _L0_attn_in['qk_ln_g'], 'L0_attn_qk_ln_b': _L0_attn_in['qk_ln_b'], 'L0_attn_qk_w': _L0_attn_in['qk_w'], 'L0_attn_qk_b': _L0_attn_in['qk_b'], 'L0_attn_qk_cw': _L0_attn_in['qk_cw'], 'L0_attn_qk_cb': _L0_attn_in['qk_cb'], 'L0_attn_out_ln_g': _L0_attn_in['out_ln_g'], 'L0_attn_out_ln_b': _L0_attn_in['out_ln_b'], 'L0_attn_out_w': _L0_attn_in['out_w'], 'L0_attn_out_b': _L0_attn_in['out_b'], 'L0_attn_out_cw': _L0_attn_in['out_cw'], 'L0_attn_out_cb': _L0_attn_in['out_cb'], 'L0_attn_gamma': _L0_attn_in['gamma'], 'L0_attn_beta': _L0_attn_in['beta'], 'L0_ffn_Wr': _L0_ffn_in['Wr'], 'L0_ffn_sWg': _L0_ffn_in['sWg'], 'L0_ffn_sWu': _L0_ffn_in['sWu'], 'L0_ffn_sWd': _L0_ffn_in['sWd'], 'L0_ffn_Wg': _L0_ffn_in['Wg'], 'L0_ffn_Wu': _L0_ffn_in['Wu'], 'L0_ffn_Wd': _L0_ffn_in['Wd']}

def reference(x, L0_tok_W, L0_tok_b, L0_attn_u_ln_g, L0_attn_u_ln_b, L0_attn_u_w, L0_attn_u_b, L0_attn_u_cw, L0_attn_u_cb, L0_attn_v_ln_g, L0_attn_v_ln_b, L0_attn_v_w, L0_attn_v_b, L0_attn_v_cw, L0_attn_v_cb, L0_attn_qk_ln_g, L0_attn_qk_ln_b, L0_attn_qk_w, L0_attn_qk_b, L0_attn_qk_cw, L0_attn_qk_cb, L0_attn_out_ln_g, L0_attn_out_ln_b, L0_attn_out_w, L0_attn_out_b, L0_attn_out_cw, L0_attn_out_cb, L0_attn_gamma, L0_attn_beta, L0_ffn_Wr, L0_ffn_sWg, L0_ffn_sWu, L0_ffn_sWd, L0_ffn_Wg, L0_ffn_Wu, L0_ffn_Wd):
    import jax
    import jax.numpy as jnp

    def _L0_tok_ref(x, W, b, chunk_size):
        import jax, jax.numpy as jnp
        import numpy as np
        B, S, D = (4, 8192, 128)
        CHUNK = 16
        Bq, Sq, Dq = x.shape
        n = Sq // chunk_size
        xr = x.reshape(Bq, n, chunk_size, Dq)
        logits = jnp.einsum('bncd,ed->bnce', xr, W) + b
        attn = jax.nn.softmax(logits, axis=-2)
        return jnp.sum(xr * attn, axis=-2)

    def _L0_attn_ref(x, u_ln_g, u_ln_b, u_w, u_b, u_cw, u_cb, v_ln_g, v_ln_b, v_w, v_b, v_cw, v_cb, qk_ln_g, qk_ln_b, qk_w, qk_b, qk_cw, qk_cb, out_ln_g, out_ln_b, out_w, out_b, out_cw, out_cb, gamma, beta):
        import jax, jax.numpy as jnp
        import numpy as np
        B, T, D = (4, 1024, 128)
        H = 256
        QK = 128
        G = 64

        def _conv_module(x, ln_g, ln_b, w, b, cw, cb):
            mu = jnp.mean(x, axis=-1, keepdims=True)
            var = jnp.mean(jnp.square(x - mu), axis=-1, keepdims=True)
            xn = (x - mu) * jax.lax.rsqrt(var + 1e-05) * ln_g + ln_b
            h = jax.nn.silu(xn @ w + b)
            hp = jnp.pad(h, ((0, 0), (1, 1), (0, 0)))
            conv = hp[:, :-2] * cw[:, 0] + hp[:, 1:-1] * cw[:, 1] + hp[:, 2:] * cw[:, 2] + cb
            return h + conv

        def _rotary(x):
            b, n, d = x.shape
            inv_freq = 1.0 / 10000.0 ** (jnp.arange(0, d, 2, dtype=jnp.float32) / d)
            freqs = jnp.arange(n, dtype=jnp.float32)[:, None] * inv_freq
            emb = jnp.repeat(freqs, 2, axis=-1)
            cos, sin = (jnp.cos(emb), jnp.sin(emb))
            xp = x.reshape(b, n, d // 2, 2)
            rot = jnp.stack([-xp[..., 1], xp[..., 0]], axis=-1).reshape(b, n, d)
            return x * cos + rot * sin

        def _forward(x, u_ln_g, u_ln_b, u_w, u_b, u_cw, u_cb, v_ln_g, v_ln_b, v_w, v_b, v_cw, v_cb, qk_ln_g, qk_ln_b, qk_w, qk_b, qk_cw, qk_cb, out_ln_g, out_ln_b, out_w, out_b, out_cw, out_cb, gamma, beta):
            seq_len = x.shape[1]
            u = _conv_module(x, u_ln_g, u_ln_b, u_w, u_b, u_cw, u_cb)
            v = _conv_module(x, v_ln_g, v_ln_b, v_w, v_b, v_cw, v_cb)
            z = _conv_module(x, qk_ln_g, qk_ln_b, qk_w, qk_b, qk_cw, qk_cb)
            qk4 = z[..., None, :] * gamma + beta
            quad_q = _rotary(qk4[:, :, 0])
            lin_q = _rotary(qk4[:, :, 1])
            quad_k = _rotary(qk4[:, :, 2])
            lin_k = _rotary(qk4[:, :, 3])
            lin_kv = jnp.einsum('bnd,bne->bde', lin_k, v) / seq_len
            lin_ku = jnp.einsum('bnd,bne->bde', lin_k, u) / seq_len
            lin_out_v = jnp.einsum('bnd,bde->bne', lin_q, lin_kv)
            lin_out_u = jnp.einsum('bnd,bde->bne', lin_q, lin_ku)
            pad = -seq_len % G

            def grp(t):
                if pad:
                    t = jnp.pad(t, ((0, 0), (0, pad), (0, 0)))
                return t.reshape(t.shape[0], -1, G, t.shape[-1])
            qq, qk_, ug, vg = (grp(quad_q), grp(quad_k), grp(u), grp(v))
            sim = jnp.einsum('bnid,bnjd->bnij', qq, qk_) / G
            attn = jnp.square(jax.nn.relu(sim))
            quad_out_v = jnp.einsum('bnij,bnjd->bnid', attn, vg).reshape(x.shape[0], -1, vg.shape[-1])[:, :seq_len]
            quad_out_u = jnp.einsum('bnij,bnjd->bnid', attn, ug).reshape(x.shape[0], -1, ug.shape[-1])[:, :seq_len]
            v_hat = quad_out_v + lin_out_v
            u_hat = quad_out_u + lin_out_u
            o_gate = jax.nn.sigmoid(u * v_hat)
            gated = u_hat * v * o_gate
            return _conv_module(gated, out_ln_g, out_ln_b, out_w, out_b, out_cw, out_cb) + x
        return _forward(x, u_ln_g, u_ln_b, u_w, u_b, u_cw, u_cb, v_ln_g, v_ln_b, v_w, v_b, v_cw, v_cb, qk_ln_g, qk_ln_b, qk_w, qk_b, qk_cw, qk_cb, out_ln_g, out_ln_b, out_w, out_b, out_cw, out_cb, gamma, beta)

    def _L0_ffn_ref(hidden_states, Wr, sWg, sWu, sWd, Wg, Wu, Wd):
        import jax, jax.numpy as jnp
        import numpy as np
        E = 64
        K = 6
        NS = 2
        D = 128
        F = 128

        def _swiglu_ffn(x, wg, wu, wd):
            return jax.nn.silu(x @ wg) * (x @ wu) @ wd
        B, S, d = hidden_states.shape
        x = hidden_states.reshape(-1, d)
        N = x.shape[0]
        shared = jnp.zeros_like(x)
        for e in range(NS):
            shared = shared + _swiglu_ffn(x, sWg[e], sWu[e], sWd[e])
        logits = x @ Wr
        probs = jax.nn.softmax(logits, axis=-1)
        top_w, top_i = jax.lax.top_k(probs, K)
        top_w = top_w / jnp.sum(top_w, axis=-1, keepdims=True)
        gate = jnp.zeros((N, E), dtype=x.dtype).at[jnp.arange(N)[:, None], top_i].set(top_w)
        routed = jnp.zeros_like(x)
        for e in range(E):
            routed = routed + _swiglu_ffn(x, Wg[e], Wu[e], Wd[e]) * gate[:, e:e + 1]
        out = (shared + routed + x).reshape(B, S, d)
        return out
    h = _L0_tok_ref(x, L0_tok_W, L0_tok_b, 16)
    h = h + _L0_attn_ref(_layernorm(h, axis=-1), L0_attn_u_ln_g, L0_attn_u_ln_b, L0_attn_u_w, L0_attn_u_b, L0_attn_u_cw, L0_attn_u_cb, L0_attn_v_ln_g, L0_attn_v_ln_b, L0_attn_v_w, L0_attn_v_b, L0_attn_v_cw, L0_attn_v_cb, L0_attn_qk_ln_g, L0_attn_qk_ln_b, L0_attn_qk_w, L0_attn_qk_b, L0_attn_qk_cw, L0_attn_qk_cb, L0_attn_out_ln_g, L0_attn_out_ln_b, L0_attn_out_w, L0_attn_out_b, L0_attn_out_cw, L0_attn_out_cb, L0_attn_gamma, L0_attn_beta)
    h = h + _L0_ffn_ref(_layernorm(h, axis=-1), L0_ffn_Wr, L0_ffn_sWg, L0_ffn_sWu, L0_ffn_sWd, L0_ffn_Wg, L0_ffn_Wu, L0_ffn_Wd)
    return h

_drawn_inputs = setup_inputs


def setup_inputs(seed=0):
    import zlib

    import numpy as np

    out = dict(_drawn_inputs(seed))
    spreads = {'L0_tok_b': (0.0, 2.0),
     'L0_attn_u_ln_g': (1.0, 0.6),
     'L0_attn_u_ln_b': (0.0, 0.595),
     'L0_attn_u_b': (0.0, 0.1),
     'L0_attn_u_cb': (0.0, 0.1),
     'L0_attn_v_ln_g': (1.0, 0.6),
     'L0_attn_v_ln_b': (0.0, 0.8),
     'L0_attn_v_b': (0.0, 0.1),
     'L0_attn_v_cb': (0.0, 0.1),
     'L0_attn_qk_ln_g': (1.0, 0.6),
     'L0_attn_qk_ln_b': (0.0, 0.8),
     'L0_attn_qk_b': (0.0, 0.8),
     'L0_attn_qk_cb': (0.0, 0.694),
     'L0_attn_out_ln_g': (1.0, 0.6),
     'L0_attn_out_ln_b': (0.0, 0.636),
     'L0_attn_out_b': (0.0, 0.1),
     'L0_attn_out_cb': (0.0, 0.1),
     'L0_attn_beta': (0.0, 2.0)}
    factors = {'L0_attn_u_cw': 8.0,
     'L0_attn_v_cw': 8.0,
     'L0_attn_qk_w': 8.0,
     'L0_attn_qk_cw': 8.0,
     'L0_attn_out_cw': 8.0,
     'L0_attn_gamma': 64.0,
     'L0_ffn_Wr': 8.0,
     'L0_ffn_sWg': 8.0,
     'L0_ffn_sWu': 8.0,
     'L0_ffn_sWd': 8.0,
     'L0_ffn_Wg': 8.0,
     'L0_ffn_Wu': 8.0,
     'L0_ffn_Wd': 8.0}
    for name, (base, spread) in spreads.items():
        noise = np.random.default_rng([zlib.crc32(name.encode()), seed]).standard_normal(out[name].shape)
        drawn = base * np.exp(spread * noise) if base else spread * noise
        out[name] = jnp.asarray(drawn.astype(out[name].dtype))
    for name, factor in factors.items():
        out[name] = (out[name] * factor).astype(out[name].dtype)
    return out
```

```python
import math

import numpy as np

import concourse.bass as bass
from concourse import mybir
from contextlib import ExitStack

F32 = mybir.dt.float32
BF16 = mybir.dt.bfloat16
U32 = mybir.dt.uint32
I32 = mybir.dt.int32
ALU = mybir.AluOpType
ACT = mybir.ActivationFunctionType
AX = mybir.AxisListType

P = 128
B, S, D = 8, 8192, 128
CHUNK = 16
T = S // CHUNK
N = B * T
H = 256
G = 64
NE, NS, K = 64, 2, 6
F = 128
TJ = T // P
EPS = 1e-5

PAR = {}
_at = 0
for _name, _n in (("tok_b", 1), ("ln_g", 3), ("ln_b", 3), ("proj_b", 5), ("cw0", 5), ("cw1", 5), ("cw2", 5),
                  ("cb", 5), ("out_g", 2), ("out_lb", 2), ("out_b", 1), ("out_cw", 3), ("out_cb", 1),
                  ("gamma", 4), ("beta", 4), ("gamma_sw", 4), ("beta_sw", 4)):
    PAR[_name] = _at
    _at += _n
NPAR = _at


def need(eng, semaphore, value):
    if not isinstance(value, int) or value > 0:
        eng.wait_ge(semaphore, value)


def pool_chunks(nc, mem, sem, x_dram, w_dram):
    SUPER, UNITS = 2048, 4
    NSUPER = B * S // SUPER
    A, GU = 4, 32
    hT, ident, par, wT = mem["hT"], mem["ident"], mem["par"], mem["tok_wT"]
    x_v = x_dram.rearrange("b s d -> (b s) d").rearrange("(n u p a) d -> n p u (a d)", u=UNITS, p=P, a=A)

    with ExitStack() as ctx:
        def sb(name, shape, dt=F32):
            return ctx.enter_context(nc.sbuf_tensor(name, shape, dt))

        R = 4
        xin = sb("x_in", [P, 2, UNITS, A * D])
        xT = sb("x_T", [P, 2 * R, 512])
        shifted = sb("x_shift", [P, 2, 512])
        ex = sb("x_exp", [P, R, 512])
        xe = sb("x_weighted", [P, R, 512])
        eh = sb("x_exp_halves", [P, R, GU, CHUNK // 2])
        wh = sb("x_weighted_halves", [P, R, GU, CHUNK // 2])
        mx = sb("x_max", [P, 2, GU])
        mb = sb("x_max_bias", [P, 2, GU])
        esum = sb("x_esum", [P, 2, UNITS, GU])
        wsum = sb("x_wsum", [P, 2, UNITS, GU])
        rec = sb("x_rec", [P, 2, UNITS, GU])
        psX = [ctx.enter_context(nc.psum_tensor(f"ps_xT{i}", [P, 512], F32)) for i in range(2)]
        psL = [ctx.enter_context(nc.psum_tensor(f"ps_logit{i}", [P, 512], F32)) for i in range(R)]
        block = ctx.enter_context(nc.Block())
        b_tok = par[:, PAR["tok_b"]:PAR["tok_b"] + 1]

        loaded = [sem(f"x_loaded{i}") for i in range(2)]
        transposed, copied, logits = sem("x_transposed"), sem("x_copied"), sem("x_logits")
        maxed, biased, subtracted, exped = sem("x_maxed"), sem("x_biased"), sem("x_subtracted"), sem("x_exped")
        weighted, esummed, wsummed = sem("x_weighted_ok"), sem("x_esummed"), sem("x_wsummed")
        ehalved, whalved, inverted, pooled = sem("x_ehalved"), sem("x_whalved"), sem("x_inverted"), sem("x_pooled")
        LAST = NSUPER * UNITS - 1
        POOL_HALVES = (0,)

        HALVED = UNITS // len(POOL_HALVES)

        def whalved_by(u, v):
            return u - v % UNITS + HALVED * sum(w <= v % UNITS for w in POOL_HALVES)

        def pipeline(eng, lag, steps):
            def turn(u, v):
                for lag, step in steps:
                    w = u - lag
                    if not isinstance(u, int) or 0 <= w <= LAST:
                        step(w, (v - lag) % (2 * UNITS))
            for u in range(4 * UNITS):
                turn(u, u % (2 * UNITS))
            with eng.Fori(2, NSUPER // 2) as i:
                for v in range(2 * UNITS):
                    turn(i * (2 * UNITS) + v, v)
            for u in range(LAST + 1, LAST + 1 + lag):
                turn(u, u % (2 * UNITS))

        @block.sync
        def _(sp):
            for n in range(2):
                sp.dma_start(xin[:, n], x_v[n]).then_inc(loaded[n], 16)
            with sp.Fori(1, NSUPER // 2) as i:
                for n in range(2):
                    sp.wait_ge(transposed, (i * 2 + n - 1) * UNITS)
                    sp.dma_start(xin[:, n], x_v[bass.ds(i * 2 + n, 1)].rearrange("o p u k -> (o p) u k"))\
                      .then_inc(loaded[n], 16)

        @block.tensor
        def _(pe):
            def transposes(u, v):
                n, k = v // UNITS, v % UNITS
                if k == 0:
                    if isinstance(u, int):
                        pe.wait_ge(loaded[n], 16 * (u // (2 * UNITS) + 1))
                    else:
                        pe.wait_ge(loaded[n], (u - v) * (16 // (2 * UNITS)) + 16)
                need(pe, copied, u - 1)
                for a in range(A):
                    mm = nc.tensor.transpose(psX[v % 2][:, a * P:(a + 1) * P],
                                             xin[:, n, k, a * D:(a + 1) * D], ident[:, :])
                mm.then_inc(transposed, 1)

            def project(u, v):
                pe.wait_ge(copied, u + 1)
                need(pe, subtracted, u - (R - 1))
                nc.tensor.matmul(psL[v % R][:, :], wT[:, :], xT[:, v, :], start=True, stop=True)\
                  .then_inc(logits, 1)
            pipeline(pe, 1, ((0, transposes), (1, project)))

        @block.scalar
        def _(act):
            def copy(u, v):
                act.wait_ge(transposed, u + 1)
                need(act, weighted, u - (2 * R - 1))
                nc.scalar.activation(xT[:, v, :].rearrange("d (g a q) -> d a g q", g=GU, a=A),
                                     psX[v % 2][:, :].rearrange("d (a g q) -> d a g q", a=A, g=GU),
                                     ACT.Copy).then_inc(copied, 1)

            def add_bias(u, v):
                act.wait_ge(maxed, u + 1)
                need(act, subtracted, u - 1)
                nc.scalar.activation(mb[:, v % 2, :], mx[:, v % 2, :], ACT.Identity, bias=b_tok).then_inc(biased, 1)

            def exp(u, v):
                act.wait_ge(subtracted, u + 1)
                need(act, ehalved, u - (R - 1))
                nc.scalar.activation(ex[:, v % R, :], shifted[:, v % 2, :], ACT.Exp, bias=b_tok).then_inc(exped, 1)
            pipeline(act, 3, ((0, copy), (3, exp), (2, add_bias)))

        @block.gpsimd
        def _(pool):
            def weigh(u, v):
                pool.wait_ge(exped, u + 1)
                need(pool, wsummed, u - (R - 1))
                nc.gpsimd.tensor_tensor(xe[:, v % R, :], xT[:, v, :], ex[:, v % R, :], ALU.mult)\
                  .then_inc(weighted, 1)
                need(pool, esummed, u - (R - 1))
                e3 = ex[:, v % R, :].rearrange("d (g c) -> d g c", g=GU)
                nc.gpsimd.tensor_tensor(eh[:, v % R], e3[:, :, 0:CHUNK // 2], e3[:, :, CHUNK // 2:], ALU.add)\
                  .then_inc(ehalved, 1)
                if v % UNITS in POOL_HALVES:
                    pool.wait_ge(weighted, u + 1)
                    x3 = xe[:, v % R, :].rearrange("d (g c) -> d g c", g=GU)
                    nc.gpsimd.tensor_tensor(wh[:, v % R], x3[:, :, 0:CHUNK // 2], x3[:, :, CHUNK // 2:], ALU.add)\
                      .then_inc(whalved, HALVED)
            def scale(u, v):
                if v % UNITS != UNITS - 1:
                    return
                n = v // UNITS
                pool.wait_ge(inverted, u + 1)
                nc.gpsimd.tensor_tensor(hT[:, bass.ds((u - (UNITS - 1)) * GU, UNITS * GU)],
                                        wsum[:, n].rearrange("d u g -> d (u g)"),
                                        rec[:, n].rearrange("d u g -> d (u g)"), ALU.mult).then_inc(pooled, UNITS)
            pipeline(pool, 6, ((3, weigh), (6, scale)))
            pool.wait_ge(pooled, LAST + 1)

        @block.vector
        def _(dve):
            def maximum(u, v):
                dve.wait_ge(logits, u + 1)
                need(dve, biased, u - 1)
                nc.vector.tensor_reduce(mx[:, v % 2, :], psL[v % R][:, :].rearrange("d (g c) -> d g c", g=GU),
                                        AX.X, ALU.max).then_inc(maxed, 1)

            def subtract(u, v):
                dve.wait_ge(biased, u + 1)
                need(dve, exped, u - 1)
                nc.vector.tensor_tensor(shifted[:, v % 2, :].rearrange("d (g c) -> d g c", g=GU),
                                        psL[v % R][:, :].rearrange("d (g c) -> d g c", g=GU),
                                        mb[:, v % 2, :].unsqueeze(2).to_broadcast([P, GU, CHUNK]),
                                        ALU.subtract).then_inc(subtracted, 1)

            def sums(u, v):
                n, k = v // UNITS, v % UNITS
                dve.wait_ge(ehalved, u + 1)
                if k == 0:
                    need(dve, pooled, u - v % UNITS - UNITS)
                nc.vector.tensor_reduce(esum[:, n, k, :], eh[:, v % R], AX.X, ALU.add).then_inc(esummed, 1)
                if k in POOL_HALVES:
                    dve.wait_ge(whalved, whalved_by(u, v))
                    src = wh[:, v % R]
                else:
                    dve.wait_ge(weighted, u + 1)
                    src = xe[:, v % R, :].rearrange("d (g c) -> d g c", g=GU)
                nc.vector.tensor_reduce(wsum[:, n, k, :], src, AX.X, ALU.add).then_inc(wsummed, 1)


            def invert(u, v):
                if v % UNITS != UNITS - 1:
                    return
                n = v // UNITS
                dve.wait_ge(wsummed, u + 1)
                need(dve, pooled, u - v % UNITS - UNITS)
                nc.vector.reciprocal(rec[:, n], esum[:, n]).then_inc(inverted, UNITS)
            pipeline(dve, 6, ((1, maximum), (2, subtract), (5, sums), (6, invert)))



def batch_pipeline(eng, s1, s2, s3, order):
    def turn(i, parity):
        for stage, step in order:
            b = i - (stage - 1)
            if isinstance(b, int) and not 0 <= b < B:
                continue
            fn = (s1, s2, s3)[stage - 1].get(step[0])
            if fn is not None:
                fn(b, (parity + stage - 1) % 2, *map(int, step[1:]))

    for i in range(4):
        turn(i, i % 2)
    with eng.Fori(2, B // 2) as t:
        turn(t * 2, 0)
        turn(t * 2 + 1, 1)
    for i in range(B, B + 2):
        turn(i, i % 2)


ORDER = [(2, f"a{k}") for k in range(5)] + \
    [(2, "b0"), (2, "b1"), (3, "a"), (2, "b2"), (2, "b3"), (3, "b0"), (3, "b1"), (2, "b4"),
     (1, "a"), (3, "c"), (1, "b"), (1, "c"), (3, "d")]

U0, V0, LK = 0, 2, 4
QQ, LQ, QK, KL = range(4)


def attention(nc, mem, sem, projw_d, outw_d, cos_d, sin_d):
    hT, ident, par = mem["hT"], mem["ident"], mem["par"]

    def pc(name, k=0):
        return par[:, PAR[name] + k:PAR[name] + k + 1]

    with ExitStack() as ctx:
        def sb(name, shape, dt=F32):
            return ctx.enter_context(nc.sbuf_tensor(name, shape, dt))

        wraw = sb("proj_raw", [P, 5 * P])
        owraw = sb("out_raw", [P, 2, P])
        w = sb("proj_w_sb", [P, 5 * P])
        ow = sb("out_w_sb", [P, 2, P])
        pb = sb("proj_bias", [P, 6])
        cw1 = sb("conv_mid", [P, 6])
        cos, sin = sb("cos_sb", [P, T]), sb("sin_sb", [P, T])
        mhalf, eps = sb("minus_half", [P, TJ]), sb("eps", [P, TJ])
        hcur = sb("h_cur", [P, T])
        spare = sb("spare", [1, 1])
        xn = sb("h_norm_tok", [P, TJ, P])
        y = sb("h_norm2_tok", [P, TJ, P])
        st = [sb(f"ln_stats{n}", [P, TJ, 6]) for n in range(3)]
        mv = [sb(f"ln_mv{n}", [P, TJ, 2]) for n in range(3)]
        ve = [sb(f"ln_var{n}", [P, TJ]) for n in range(3)]
        rs = [sb(f"ln_rstd{n}", [P, TJ]) for n in range(3)]
        yT = sb("y_T", [P, 2, T])
        hb = sb("silu_rows", [P, 2, 5, T + 2])
        cv = sb("conv_rows", [P, 2, 5, T])
        zs = sb("z_swapped", [P, 2, T])
        ra, rb = sb("rot_a", [P, 2, T]), sb("rot_b", [P, 2, T])
        rc, rd = sb("rot_c", [P, 2, T]), sb("rot_d", [P, 2, T])
        q4 = sb("qk_rows", [P, 2, 4, T])
        tok = sb("tok_major", [P, 2, 5, TJ, P])
        at = sb("attn_T", [P, TJ, P])
        lkv = sb("lin_kv", [P, 4, P])
        um, th, pr = sb("gate_arg", [P, 2, T]), sb("gate_tanh", [P, 2, T]), sb("gate_prod", [P, 2, T])
        gt = sb("gated", [P, 2, T])
        gn = sb("gated_norm_tok", [P, TJ, H])
        gT = sb("gated_norm_T", [P, 2, T])
        ho = sb("out_silu", [P, T + 2])
        oc = sb("out_conv", [P, T])

        def ps(name):
            return ctx.enter_context(nc.psum_tensor(name, [P, 512], F32))

        with ExitStack() as setup:
            psB = setup.enter_context(nc.psum_tensor("ps_bias", [P, 512], F32))
            block = setup.enter_context(nc.Block())
            w_loaded, folded, bias_mm, biased = sem("w_loaded"), sem("w_folded"), sem("bias_mm"), sem("bias_added")
            cleared, halved = sem("rows_cleared"), sem("gamma_scaled")

            @block.sync
            def _(sp):
                sp.dma_start(wraw[:, :], projw_d).then_inc(w_loaded, 16)
                sp.dma_start(owraw[:, :, :], outw_d).then_inc(w_loaded, 16)
                sp.dma_start(cos[:, :], cos_d).then_inc(w_loaded, 16)
                sp.dma_start(sin[:, :], sin_d).then_inc(w_loaded, 16)

            @block.gpsimd
            def _(pool):
                nc.gpsimd.memset(hb[:, :, :, 0:1], 0.0).then_inc(cleared, 1)
                nc.gpsimd.memset(hb[:, :, :, T + 1:T + 2], 0.0).then_inc(cleared, 1)
                nc.gpsimd.memset(ho[:, 0:1], 0.0).then_inc(cleared, 1)
                nc.gpsimd.memset(ho[:, T + 1:T + 2], 0.0).then_inc(cleared, 1)
                nc.gpsimd.memset(at[:, :, :], 0.0).then_inc(cleared, 1)
                nc.gpsimd.memset(mhalf[:, :], -0.5).then_inc(cleared, 1)
                nc.gpsimd.memset(eps[:, :], EPS).then_inc(cleared, 1)
                pool.wait_ge(cleared, 7)

            @block.tensor
            def _(pe):
                pe.wait_ge(w_loaded, 64)
                for c in range(5):
                    nc.tensor.matmul(psB[:, c:c + 1], wraw[:, c * P:(c + 1) * P], pc("ln_b", c // 2),
                                     start=True, stop=True)
                for f in range(2):
                    mm = nc.tensor.matmul(psB[:, 5:6], owraw[:, f, :], pc("out_lb", f), start=(f == 0), stop=(f == 1))
                mm.then_inc(bias_mm, 1)

            @block.vector
            def _(dve):
                dve.wait_ge(w_loaded, 64)
                for c in range(5):
                    nc.vector.tensor_scalar(w[:, c * P:(c + 1) * P], wraw[:, c * P:(c + 1) * P], pc("ln_g", c // 2),
                                            None, ALU.mult).then_inc(folded, 1)
                for f in range(2):
                    nc.vector.tensor_scalar(ow[:, f, :], owraw[:, f, :], pc("out_g", f), None, ALU.mult)\
                      .then_inc(folded, 1)
                nc.vector.tensor_scalar(cw1[:, 0:5], par[:, PAR["cw1"]:PAR["cw1"] + 5], 1.0, None, ALU.add)\
                  .then_inc(folded, 1)
                nc.vector.tensor_scalar(cw1[:, 5:6], pc("out_cw", 1), 1.0, None, ALU.add).then_inc(folded, 1)
                for name in ("gamma", "beta", "gamma_sw", "beta_sw"):
                    nc.vector.tensor_scalar(pc(name, QQ), pc(name, QQ), 1.0 / G, None, ALU.mult).then_inc(halved, 1)
                dve.wait_ge(bias_mm, 1)
                nc.vector.tensor_tensor(pb[:, 0:5], psB[:, 0:5], par[:, PAR["proj_b"]:PAR["proj_b"] + 5], ALU.add)\
                  .then_inc(biased, 1)
                nc.vector.tensor_tensor(pb[:, 5:6], psB[:, 5:6], pc("out_b"), ALU.add).then_inc(biased, 1)
                dve.wait_ge(folded, 9)
                dve.wait_ge(halved, 4)
                dve.wait_ge(biased, 2)

        psT, psR = ps("ps_ln_in"), ps("ps_ln_out")
        ring = [ps(f"ps_ring{n}") for n in range(2)]
        psQ = [ps(f"ps_out{n}") for n in range(4)]
        block = ctx.enter_context(nc.Block())

        h_taken = sem("h_taken")
        h_tok = sem("h_tok")
        stats = [sem(f"ln{n}_stats") for n in range(3)]
        aggr = [sem(f"ln{n}_aggr") for n in range(3)]
        var_eps = [sem(f"ln{n}_var_eps") for n in range(3)]
        rstd = [sem(f"ln{n}_rstd") for n in range(3)]
        norm = [sem(f"ln{n}_norm") for n in range(3)]
        xn_back, based = sem("xn_back"), sem("h_based")
        y_back, y_copied = sem("y_back"), sem("y_copied")
        ring_full, ring_used = sem("ring_full"), sem("ring_used")
        mid, left, conv = sem("conv_mid_done"), sem("conv_left"), sem("conv_done")
        swapped, rot_in, rot_c, rot_d, rotated = (sem("z_swapped_ok"), sem("rot_in"), sem("rot_cos"),
                                                 sem("rot_sin"), sem("rotated"))
        sims, attned, kv_mm, kv_copied = sem("sims"), sem("attned"), sem("kv_mm"), sem("kv_copied")
        hats, gate_arg, gate_tanh, gate_prod, gated = (sem("hats"), sem("gate_arg_ok"), sem("gate_tanh_ok"),
                                                      sem("gate_prod_ok"), sem("gated_ok"))
        g_tok, g_back, g_copied = sem("g_tok"), sem("g_back"), sem("g_copied")
        o_mm, o_silu, o_mid, o_left, o_conv, added = (sem("o_mm"), sem("o_silu"), sem("o_mid"), sem("o_left"),
                                                     sem("o_conv"), sem("h_added"))
        CORD = [4, 0, 1, 2, 3]

        @block.tensor
        def _(pe):
            def s1a(b, q):
                pe.wait_ge(h_taken, b + 1)
                need(pe, norm[0], b)
                for j in range(TJ):
                    mm = nc.tensor.transpose(psT[:, j * P:(j + 1) * P], hcur[:, j * P:(j + 1) * P], ident[:, :])
                mm.then_inc(h_tok, 1)

            def s1b(b, q):
                pe.wait_ge(norm[0], b + 1)
                need(pe, y_copied, b)
                for j in range(TJ):
                    mm = nc.tensor.transpose(psR[:, j * P:(j + 1) * P], xn[:, j, :], ident[:, :])
                mm.then_inc(xn_back, 1)

            def s1c(b, q):
                pe.wait_ge(norm[1], b + 1)
                pe.wait_ge(based, b + 1)
                for j in range(TJ):
                    mm = nc.tensor.transpose(psR[:, j * P:(j + 1) * P], y[:, j, :], ident[:, :])
                mm.then_inc(y_back, 1)

            def s2a(b, q, k):
                c = CORD[k]
                if k == 0:
                    pe.wait_ge(y_copied, b + 1)
                need(pe, ring_used, b * 10 + (k - 1))
                nc.tensor.matmul(ring[k % 2][:, :], w[:, c * P:(c + 1) * P], yT[:, q, :], start=True, stop=True)\
                  .then_inc(ring_full, 1)

            def s2b(b, q, k):
                for c in (k,):
                    if c == LK:
                        pe.wait_ge(rotated, b * 4 + 4)
                    else:
                        pe.wait_ge(conv, b * 5 + CORD.index(c) + 1)
                    pe.wait_ge(ring_used, b * 10 + 4 + k)
                    src = q4[:, q, KL, :] if c == LK else cv[:, q, c, :]
                    for j in range(TJ):
                        mm = nc.tensor.transpose(ring[(5 + k) % 2][:, j * P:(j + 1) * P], src[:, j * P:(j + 1) * P],
                                                 ident[:, :])
                    mm.then_inc(ring_full, 1)

            def s3a(b, q):
                pe.wait_ge(rotated, b * 4 + 4)
                need(pe, o_silu, b)
                for j in range(TJ):
                    mm = nc.tensor.matmul(psQ[0][:, j * P:(j + 1) * P], q4[:, q, QK, j * P:(j + 1) * P],
                                          q4[:, q, QQ, j * P:(j + 1) * P], start=True, stop=True)
                mm.then_inc(sims, 1)
                pe.wait_ge(ring_used, b * 10 + 10)
                for j in range(TJ):
                    mm = nc.tensor.matmul(psQ[1][:, :], tok[:, q, LK, j, :], tok[:, q, 0:4, j, :],
                                          start=(j == 0), stop=(j == TJ - 1))
                mm.then_inc(kv_mm, 1)

            def s3b(b, q, m):
                if m == 0:
                    pe.wait_ge(attned, b + 1)
                    pe.wait_ge(kv_copied, b + 1)
                for c in ((V0, V0 + 1), (U0, U0 + 1))[m]:
                    for j in range(TJ):
                        nc.tensor.matmul(psQ[c][:, j * P:(j + 1) * P], tok[:, q, c, j, :], at[:, j, :],
                                         start=(j == 0), stop=False, skip_group_check=True)
                    mm = nc.tensor.matmul(psQ[c][:, :], lkv[:, c, :], q4[:, q, LQ, :], start=False, stop=True,
                                          skip_group_check=True)
                    mm.then_inc(hats, 1)

            def s3c(b, q):
                pe.wait_ge(gated, b * 2 + 2)
                for j in range(TJ):
                    for f in range(2):
                        mm = nc.tensor.transpose(psQ[j // 2][:, (j % 2) * H + f * P:(j % 2) * H + (f + 1) * P],
                                                 gt[:, f, j * P:(j + 1) * P], ident[:, :])
                mm.then_inc(g_tok, 1)
                pe.wait_ge(norm[2], b + 1)
                for f in range(2):
                    for j in range(TJ):
                        mm = nc.tensor.transpose(psQ[2 + f][:, j * P:(j + 1) * P], gn[:, j, f * P:(f + 1) * P],
                                                 ident[:, :])
                    mm.then_inc(g_back, 1)

            def s3d(b, q):
                pe.wait_ge(g_copied, b * 2 + 2)
                for f in range(2):
                    mm = nc.tensor.matmul(psQ[0][:, :], ow[:, f, :], gT[:, f, :], start=(f == 0), stop=(f == 1))
                mm.then_inc(o_mm, 1)

            batch_pipeline(pe, {"a": s1a, "b": s1b, "c": s1c}, {"a": s2a, "b": s2b},
                           {"a": s3a, "b": s3b, "c": s3c, "d": s3d}, ORDER)

        @block.scalar
        def _(act):
            def s1c(b, q):
                act.wait_ge(y_back, b + 1)
                need(act, ring_full, (b - 1) * 10 - 5)
                nc.scalar.activation(yT[:, q, :], psR[:, :], ACT.Copy).then_inc(y_copied, 1)

            def s2a(b, q, k):
                def middle(k, c):
                    act.wait_ge(ring_used, b * 10 + k + 1)
                    nc.scalar.activation(cv[:, q, c, :], hb[:, q, c, 1:T + 1], ACT.Identity, scale=cw1[:, c:c + 1],
                                         bias=pc("cb", c)).then_inc(mid, 1)

                if k == 0:
                    need(act, hats, (b - 1) * 4)
                    need(act, gated, (b - 1) * 2)
                    need(act, ring_used, (b - 1) * 10)
                    need(act, ring_full, (b - 1) * 10)
                    need(act, conv, (b - 1) * 5)
                    need(act, rotated, (b - 1) * 4)
                c = CORD[k]
                act.wait_ge(ring_full, b * 10 + k + 1)
                nc.scalar.activation(hb[:, q, c, 1:T + 1], ring[k % 2][:, :], ACT.Silu, bias=pb[:, c:c + 1])\
                  .then_inc(ring_used, 1)
                if k:
                    middle(k - 1, CORD[k - 1])
                if k == 4:
                    middle(4, CORD[4])

            def s2b(b, q, k):
                def rot(i):
                    if i == 0:
                        act.wait_ge(conv, b * 5 + 1)
                        act.wait_ge(swapped, b + 1)
                    need(act, rot_c, b * 4 + i - 1)
                    need(act, rot_d, b * 4 + i - 1)
                    nc.scalar.activation(ra[:, i % 2, :], cv[:, q, 4, :], ACT.Identity, scale=pc("gamma", i),
                                         bias=pc("beta", i)).then_inc(rot_in, 1)
                    nc.scalar.activation(rb[:, i % 2, :], zs[:, q, :], ACT.Identity, scale=pc("gamma_sw", i),
                                         bias=pc("beta_sw", i)).then_inc(rot_in, 1)

                def to_tok(k, c):
                    act.wait_ge(ring_full, b * 10 + 5 + k + 1)
                    nc.scalar.activation(tok[:, q, c, :, :].rearrange("p j e -> p (j e)"), ring[(5 + k) % 2][:, :],
                                         ACT.Copy).then_inc(ring_used, 1)

                if k < 4:
                    rot(k)
                to_tok(k, k)

            def s3a(b, q):
                act.wait_ge(kv_mm, b + 1)
                need(act, hats, b * 4)
                nc.scalar.activation(lkv[:, :, :].rearrange("p c e -> p (c e)"), psQ[1][:, :], ACT.Copy,
                                     scale=1.0 / T).then_inc(kv_copied, 1)

            def s3b(b, q, m):
                for f in range(2) if m == 0 else ():
                    act.wait_ge(gate_arg, b * 2 + f + 1)
                    need(act, gated, b * 2)
                    nc.scalar.activation(th[:, f, :], um[:, f, :], ACT.Tanh, scale=0.5).then_inc(gate_tanh, 1)

            def s3c(b, q):
                for f in range(2):
                    act.wait_ge(g_back, b * 2 + f + 1)
                    need(act, o_mm, b)
                    nc.scalar.activation(gT[:, f, :], psQ[2 + f][:, :], ACT.Copy).then_inc(g_copied, 1)

            def s3d(b, q):
                act.wait_ge(o_mm, b + 1)
                need(act, o_conv, b)
                nc.scalar.activation(ho[:, 1:T + 1], psQ[0][:, :], ACT.Silu, bias=pb[:, 5:6]).then_inc(o_silu, 1)
                act.wait_ge(o_silu, b + 1)
                need(act, added, b)
                nc.scalar.activation(oc[:, :], ho[:, 1:T + 1], ACT.Identity, scale=cw1[:, 5:6],
                                     bias=pc("out_cb")).then_inc(o_mid, 1)

            batch_pipeline(act, {"c": s1c}, {"a": s2a, "b": s2b}, {"a": s3a, "b": s3b, "c": s3c, "d": s3d}, ORDER)

        @block.gpsimd
        def _(pool):
            def inverse_root(n, b):
                pool.wait_ge(aggr[n], b + 1)
                nc.gpsimd.tensor_tensor(ve[n][:, :], mv[n][:, :, 1], eps[:, :], ALU.add).then_inc(var_eps[n], 1)
                pool.wait_ge(var_eps[n], b + 1)
                need(pool, norm[n], b)
                nc.gpsimd.tensor_tensor(rs[n][:, :], ve[n][:, :], mhalf[:, :], ALU.pow).then_inc(rstd[n], 1)

            def s1a(b, q):
                need(pool, h_tok, b)
                need(pool, based, b)
                nc.gpsimd.tensor_copy(hcur[:, :], hT[:, bass.ds(b * T, T)]).then_inc(h_taken, 1)
                inverse_root(0, b)

            def s1b(b, q):
                inverse_root(1, b)

            def s2b(b, q, k):
                for i in (k,) if k < 4 else ():
                    pool.wait_ge(rot_in, b * 8 + 2 * i + 2)
                    need(pool, rotated, b * 4 + i - 1)
                    nc.gpsimd.tensor_tensor(rc[:, i % 2, :], ra[:, i % 2, :], cos[:, :], ALU.mult).then_inc(rot_c, 1)

            def s3c(b, q):
                inverse_root(2, b)

            def s3d(b, q):
                pool.wait_ge(o_conv, b + 1)
                pool.wait_ge(based, b + 1)
                nc.gpsimd.tensor_tensor(hT[:, bass.ds(b * T, T)], hT[:, bass.ds(b * T, T)], oc[:, :], ALU.add)\
                  .then_inc(added, 1)
                if isinstance(b, int) and b == B - 1:
                    pool.wait_ge(added, B)

            batch_pipeline(pool, {"a": s1a, "b": s1b}, {"b": s2b}, {"c": s3c, "d": s3d}, ORDER)

        @block.vector
        def _(dve):
            def statistics(n, b, src, width):
                for j in range(TJ):
                    nc.vector.bn_stats(st[n][:, j, :], src(j)).then_inc(stats[n], 1)
                dve.wait_ge(stats[n], b * TJ + TJ)
                nc.vector.memset(spare[:, :], 0.0)
                for j in range(TJ):
                    ins = nc.vector.bn_aggr(mv[n][:, j, :], st[n][:, j, :])
                    if j == TJ - 1:
                        ins.then_inc(aggr[n], 1)

            def normalise(n, b, dst, src):
                dve.wait_ge(rstd[n], b + 1)
                for j in range(TJ):
                    ins = nc.vector.tensor_scalar(dst[:, j, :], src(j), mv[n][:, j, 0:1], rs[n][:, j:j + 1],
                                                  ALU.subtract, ALU.mult)
                ins.then_inc(norm[n], 1)

            def s1a(b, q):
                dve.wait_ge(h_tok, b + 1)
                statistics(0, b, lambda j: psT[:, j * P:(j + 1) * P], P)
                need(dve, xn_back, b)
                normalise(0, b, xn, lambda j: psT[:, j * P:(j + 1) * P])

            def s1b(b, q):
                dve.wait_ge(norm[0], b + 1)
                statistics(1, b, lambda j: xn[:, j, :], P)
                need(dve, y_back, b)
                normalise(1, b, y, lambda j: xn[:, j, :])
                dve.wait_ge(xn_back, b + 1)
                nc.vector.tensor_tensor(hT[:, bass.ds(b * T, T)], hcur[:, :], psR[:, :], ALU.add).then_inc(based, 1)

            def s2a(b, q, k):
                for c in (CORD[k],):
                    dve.wait_ge(mid, b * 5 + k + 1)
                    nc.vector.scalar_tensor_tensor(out=cv[:, q, c, :], in0=hb[:, q, c, 0:T], scalar=pc("cw0", c),
                                                   in1=cv[:, q, c, :], op0=ALU.mult, op1=ALU.add).then_inc(left, 1)
                    dve.wait_ge(left, b * 5 + k + 1)
                    nc.vector.scalar_tensor_tensor(out=cv[:, q, c, :], in0=hb[:, q, c, 2:T + 2], scalar=pc("cw2", c),
                                                   in1=cv[:, q, c, :], op0=ALU.mult, op1=ALU.add).then_inc(conv, 1)
                    if k == 0:
                        dve.wait_ge(conv, b * 5 + 1)
                        need(dve, rot_in, (b - 1) * 8)
                        nc.vector.memset(spare[:, :], 0.0)
                        nc.vector.stream_shuffle(zs[:, q, :], cv[:, q, 4, :], [i ^ 1 for i in range(32)])\
                          .then_inc(swapped, 1)

            def s2b(b, q, k):
                if k == 0:
                    need(dve, hats, (b - 1) * 4)
                    need(dve, ring_full, (b - 1) * 10)
                for i in (k,) if k < 4 else ():
                    dve.wait_ge(rot_in, b * 8 + 2 * i + 2)
                    nc.vector.tensor_tensor(rd[:, i % 2, :], rb[:, i % 2, :], sin[:, :], ALU.mult).then_inc(rot_d, 1)
                    dve.wait_ge(rot_d, b * 4 + i + 1)
                    dve.wait_ge(rot_c, b * 4 + i + 1)
                    nc.vector.tensor_tensor(q4[:, q, i, :], rc[:, i % 2, :], rd[:, i % 2, :], ALU.add)\
                      .then_inc(rotated, 1)

            def s3a(b, q):
                dve.wait_ge(sims, b + 1)
                need(dve, hats, b * 4)
                for g in range(P // G):
                    r = slice(g * G, (g + 1) * G)
                    s = psQ[0][r, :].rearrange("p (j i) -> p j i", j=TJ)[:, :, r]
                    ins = nc.vector.tensor_scalar(at[r, :, r], s, 0.0, None, ALU.max)
                    ins.then_inc(attned_half, 1)
                dve.wait_ge(attned_half, b * 2 + 2)
                for g in range(P // G):
                    r = slice(g * G, (g + 1) * G)
                    ins = nc.vector.tensor_tensor(at[r, :, r], at[r, :, r], at[r, :, r], ALU.mult)
                ins.then_inc(attned, 1)

            def s3b(b, q, m):
                for f in range(2) if m == 0 else ():
                    dve.wait_ge(hats, b * 4 + f + 1)
                    need(dve, gate_tanh, b * 2)
                    nc.vector.tensor_tensor(um[:, f, :], psQ[V0 + f][:, :], cv[:, q, U0 + f, :], ALU.mult)\
                      .then_inc(gate_arg, 1)
                for f in range(2) if m == 1 else ():
                    dve.wait_ge(hats, b * 4 + 2 + f + 1)
                    nc.vector.scalar_tensor_tensor(out=pr[:, f, :], in0=psQ[U0 + f][:, :], scalar=0.5,
                                                   in1=cv[:, q, V0 + f, :], op0=ALU.mult, op1=ALU.mult)\
                      .then_inc(gate_prod, 1)
                    dve.wait_ge(gate_prod, b * 2 + f + 1)
                    dve.wait_ge(gate_tanh, b * 2 + f + 1)
                    need(dve, g_tok, b)
                    nc.vector.scalar_tensor_tensor(out=gt[:, f, :], in0=th[:, f, :], scalar=1.0, in1=pr[:, f, :],
                                                   op0=ALU.add, op1=ALU.mult).then_inc(gated, 1)

            def s3c(b, q):
                def src(j):
                    return psQ[j // 2][:, (j % 2) * H:(j % 2 + 1) * H]
                dve.wait_ge(g_tok, b + 1)
                statistics(2, b, src, H)
                need(dve, g_back, b * 2)
                normalise(2, b, gn, src)

            def s3d(b, q):
                dve.wait_ge(o_mid, b + 1)
                nc.vector.scalar_tensor_tensor(out=oc[:, :], in0=ho[:, 0:T], scalar=pc("out_cw", 0), in1=oc[:, :],
                                               op0=ALU.mult, op1=ALU.add).then_inc(o_left, 1)
                dve.wait_ge(o_left, b + 1)
                nc.vector.scalar_tensor_tensor(out=oc[:, :], in0=ho[:, 2:T + 2], scalar=pc("out_cw", 2), in1=oc[:, :],
                                               op0=ALU.mult, op1=ALU.add).then_inc(o_conv, 1)

            attned_half = sem("attn_relu")
            batch_pipeline(dve, {"a": s1a, "b": s1b}, {"a": s2a, "b": s2b},
                           {"a": s3a, "b": s3b, "c": s3c, "d": s3d}, ORDER)


TILES = N // P
REGION = N + P
BLOCKS = -(-(-(-(N * K + NE * (P - 1)) // P)) // 4) * 4


def plan(nc, mem, sem, ctx, xs):
    base, slotx, oh, ident = mem["base"], mem["slotx"], mem["oh"], mem["ident"]
    tile_e, tile_row, sloty = mem["tile_e"], mem["tile_row"], mem["sloty"]
    HB = BLOCKS // P
    def sb(name, shape, dt=F32):
        return ctx.enter_context(nc.sbuf_tensor(name, shape, dt))

    region = sb("p_region", [P, NE])
    cnt = sb("p_count", [P, NE])
    cnti = sb("p_count_int", [P, NE], I32)
    msk = sb("p_masked_int", [P, NE], I32)
    padded = sb("p_padded", [P, NE])
    ends, starts, shift = sb("p_ends", [P, NE]), sb("p_starts", [P, NE]), sb("p_shift", [P, NE])
    zero_e = sb("p_zero_e", [P, NE])
    first = sb("p_first", [P, HB])
    iota = sb("p_iota", [P, NE])
    cmp = sb("p_cmp", [P, HB, NE])
    te, tr, valid, sh = (sb("p_" + n, [P, HB]) for n in ("te", "tr", "valid", "sh"))
    tails = sb("p_tails", [1, NE], I32)
    zeros = sb("p_zeros", [P, D])
    pk = sb("p_packed", [1, BLOCKS // 4])
    tmp = sb("p_tmp", [P, TJ * K, NE])
    yf = sb("p_yslot", [P, TJ * K])
    psP = ctx.enter_context(nc.psum_tensor("ps_plan", [P, 512], F32))
    made, chain, turned, tails_ok, tailed = (sem("p_made"), sem("p_step"), sem("p_turned"), sem("p_tails_ok"),
                                             sem("p_tailed"))
    cols = sem("p_cols_ok")
    y_masked, y_summed, y_slotted = sem("y_masked"), sem("y_summed"), sem("y_slotted")

    def on_pool(pool):
        nc.gpsimd.iota(region[:, :], [[REGION, NE]], base=0, channel_multiplier=0,
                       allow_small_or_imprecise_dtypes=True).then_inc(made, 1)
        nc.gpsimd.iota(iota[:, :], [[1, NE]], base=0, channel_multiplier=0,
                       allow_small_or_imprecise_dtypes=True).then_inc(made, 1)
        nc.gpsimd.iota(first[:, :], [[P * P, HB]], base=0, channel_multiplier=P,
                       allow_small_or_imprecise_dtypes=True).then_inc(made, 1)
        nc.gpsimd.memset(zero_e[:, :], 0.0).then_inc(made, 1)
        nc.gpsimd.memset(zeros[:, :], 0.0).then_inc(made, 1)

    def on_dve(dve):
        n = [0]

        def step(ins):
            n[0] += 1
            ins.then_inc(chain, 1)
            dve.wait_ge(chain, n[0])

        dve.wait_ge(made, 5)
        nc.vector.tensor_copy(tails[0:1, :], base[0:1, :]).then_inc(tails_ok, 1)
        step(nc.vector.tensor_tensor(cnt[:, :], base[:, :], region[:, :], ALU.subtract))
        step(nc.vector.tensor_scalar(cnt[:, :], cnt[:, :], float(P - 1), None, ALU.add))
        step(nc.vector.tensor_copy(cnti[:, :], cnt[:, :]))
        step(nc.vector.tensor_scalar(msk[:, :], cnti[:, :], -P, None, ALU.bitwise_and))
        step(nc.vector.tensor_copy(padded[:, :], msk[:, :]))
        step(nc.vector.tensor_tensor_scan(ends[:, :], padded[:, :], zero_e[:, :], 0.0, ALU.add, ALU.add))
        step(nc.vector.tensor_tensor(starts[:, :], ends[:, :], padded[:, :], ALU.subtract))
        step(nc.vector.tensor_tensor(shift[:, :], starts[:, :], region[:, :], ALU.subtract))
        f3 = first[:, :].unsqueeze(2).to_broadcast([P, HB, NE])
        step(nc.vector.tensor_tensor(cmp[:, :, :], ends[:, :].unsqueeze(1).to_broadcast([P, HB, NE]), f3,
                                     ALU.is_le))
        step(nc.vector.tensor_reduce(te[:, :], cmp[:, :, :], AX.X, ALU.add))
        step(nc.vector.tensor_scalar(valid[:, :], te[:, :], float(NE), None, ALU.is_lt))
        step(nc.vector.tensor_scalar(te[:, :], te[:, :], float(NE - 1), None, ALU.min))
        step(nc.vector.tensor_tensor(cmp[:, :, :], iota[:, :].unsqueeze(1).to_broadcast([P, HB, NE]),
                                     te[:, :].unsqueeze(2).to_broadcast([P, HB, NE]), ALU.is_equal))
        step(nc.vector.tensor_tensor(cmp[:, :, :], cmp[:, :, :],
                                     shift[:, :].unsqueeze(1).to_broadcast([P, HB, NE]), ALU.mult))
        step(nc.vector.tensor_reduce(sh[:, :], cmp[:, :, :], AX.X, ALU.add))
        step(nc.vector.tensor_tensor(tr[:, :], first[:, :], sh[:, :], ALU.subtract))
        nc.vector.tensor_tensor(tr[:, :], tr[:, :], valid[:, :], ALU.mult).then_inc(cols, 1)
        dve.wait_ge(turned, 1)
        e4 = psP[0:1, 0:BLOCKS].rearrange("o (g n) -> o g n", n=4)
        step(nc.vector.tensor_copy(pk[0:1, :], e4[:, :, 3]))
        for m in (2, 1, 0):
            step(nc.vector.scalar_tensor_tensor(out=pk[0:1, :], in0=pk[0:1, :], scalar=float(NE), in1=e4[:, :, m],
                                                op0=ALU.mult, op1=ALU.add))
        nc.vector.tensor_copy(tile_e[0:1, :], pk[0:1, :])
        step(nc.vector.tensor_copy(tile_row[0:1, :], psP[0:1, BLOCKS:2 * BLOCKS]))
        W = TJ * K

        def y_slots(b):
            need(dve, y_summed, b)
            nc.vector.tensor_tensor(tmp[:, :, :], oh[:, bass.ds(b * (W * NE), W * NE)]
                                    .rearrange("p (c e) -> p c e", e=NE),
                                    shift[:, :].unsqueeze(1).to_broadcast([P, W, NE]), ALU.mult)\
              .then_inc(y_masked, 1)
            dve.wait_ge(y_masked, b + 1)
            need(dve, y_slotted, b)
            nc.vector.tensor_reduce(yf[:, :], tmp[:, :, :], AX.X, ALU.add).then_inc(y_summed, 1)
            dve.wait_ge(y_summed, b + 1)
            nc.vector.tensor_tensor(sloty[:, bass.ds(b * W, W)], yf[:, :], slotx[:, bass.ds(b * W, W)], ALU.add)\
              .then_inc(y_slotted, 1)
        y_slots(0)
        with dve.Fori(1, B) as b:
            y_slots(b)
        dve.wait_ge(y_slotted, B)

    def on_pe(pe):
        pe.wait_ge(cols, 1)
        for m, col in enumerate((te, tr)):
            for h in range(HB):
                mm = nc.tensor.matmul(psP[0:1, m * BLOCKS + h * P:m * BLOCKS + (h + 1) * P], col[:, h:h + 1],
                                      ident[:, :], start=True, stop=True)
        mm.then_inc(turned, 1)

    def clear_tails(eng, engine, first):
        eng.wait_ge(tails_ok, 1)
        eng.wait_ge(made, 5)
        with eng.Fori(0, NE // 2 // 4) as t:
            rows = nc.values_load_multi_w_load_instructions(
                tails[0:1, bass.ds(t * 4 + first, 4)], engines=(engine,), min_val=0, max_val=NE * REGION - P)[1]
            for row in rows:
                eng.dma_start(xs[bass.ds(row, P), :], zeros[:, :]).then_inc(tailed, 16)

    def on_sp(sp):
        clear_tails(sp, mybir.EngineType.SP, 0)
        sp.wait_ge(tailed, 16 * NE)

    def on_act(act):
        clear_tails(act, mybir.EngineType.Activation, NE // 2)

    return on_pool, on_dve, on_pe, on_sp, on_act


def route(nc, mem, sem, wr_d, sgu_d, sd_d, gu_d, down_d, xs):
    hT, ident = mem["hT"], mem["ident"]
    res, wts, slotx, oh, base, gu, down = (mem[n] for n in ("res", "wts", "slotx", "oh", "base", "gu", "down"))
    with ExitStack() as ctx:
        def sb(name, shape, dt=F32):
            return ctx.enter_context(nc.sbuf_tensor(name, shape, dt))

        def ps(name):
            return ctx.enter_context(nc.psum_tensor(name, [P, 512], F32))

        wr = sb("wr_sb", [P, NE])
        sgu = sb("shared_gu_sb", [P, NS, 2, F])
        sd = sb("shared_d_sb", [P, NS, D])
        mhalf, eps = sb("r_minus_half", [P, TJ]), sb("r_eps", [P, TJ])
        hcur = sb("r_h_cur", [P, T])
        st, mv = sb("r_stats", [P, TJ, 6]), sb("r_mv", [P, TJ, 2])
        ve, rs = sb("r_var", [P, TJ]), sb("r_rstd", [P, TJ])
        spare = sb("r_spare", [1, 1])
        xf = sb("xf_tok", [P, 2, TJ, D])
        rows = sb("scatter_rows", [P, 2, TJ, D])
        xfT = sb("xf_T", [P, 2, T])
        nmax, esum, erec = sb("r_nmax", [P, TJ]), sb("r_esum", [P, TJ]), sb("r_erec", [P, TJ])
        ex, probs = sb("r_exp", [P, TJ, NE]), sb("r_probs", [P, TJ, NE])
        top, topi = sb("r_top", [P, TJ, 8]), sb("r_topi", [P, TJ, 8], U32)
        tsum, trec = sb("r_tsum", [P, TJ]), sb("r_trec", [P, TJ])
        idxf = sb("r_idxf", [P, TJ, K])
        iota = sb("r_iota", [P, NE])
        one = sb("r_onehot", [P, TJ * K, NE], BF16)
        took = sb("r_took", [P, TJ, NE], BF16)
        pos = sb("r_pos", [P, TJ, NE])
        tmp = sb("r_tmp", [P, TJ, K, NE])
        slf = sb("r_slot", [P, TJ * K])
        sli = sb("r_slot_int", [P, 2, TJ * K], I32)
        pspare = sb("r_pool_spare", [1, 1])
        before, ones = sb("r_before", [P, P], BF16), sb("r_ones", [P, P], BF16)
        sg, hs = sb("r_silu", [P, NS, T]), sb("r_hidden", [P, NS, T])
        psT, psR, psG, psK, psA, psU, psY = (ps("ps_r" + n) for n in "TRGKAUY")
        plan_pool, plan_dve, plan_pe, plan_sp, plan_act = plan(nc, mem, sem, ctx, xs)
        block = ctx.enter_context(nc.Block())

        loaded, gu_loaded = sem("r_loaded"), sem("gu_loaded")
        cleared, made = sem("r_cleared"), sem("r_made")
        h_taken, h_tok, stats, aggr, var_eps, rstd, norm = (
            sem("r_" + n) for n in ("h_taken", "h_tok", "stats_ok", "aggr", "var_eps", "rstd_ok", "norm"))
        based, back, copied, logits = sem("res_based"), sem("r_back"), sem("r_copied"), sem("r_logits")
        maxed, exped, inv, prob, topped = (sem("r_maxed"), sem("r_exped"), sem("r_inv"), sem("r_prob_ok"),
                                           sem("r_topped"))
        indexed, floated, tsummed, tinv, weighed = (sem("r_indexed"), sem("r_floated"), sem("r_tsummed"),
                                                    sem("r_tinv"), sem("r_weighed"))
        onehot, taken, ranked, placed, moved = (sem("r_onehot_ok"), sem("r_taken"), sem("r_ranked"),
                                                sem("r_placed"), sem("base_moved"))
        masked, summed, slotted, kept = sem("r_masked"), sem("r_summed"), sem("r_slotted"), sem("r_kept")
        carried, rows_copied = sem("r_carried"), sem("r_rows_copied")
        scattered = [sem(f"r_scattered{q}") for q in range(2)]
        gate_mm, up_mm, gated, hidden, shared_mm, shared_add = (
            sem("r_" + n) for n in ("gate_mm", "up_mm", "gated_ok", "hidden_ok", "shared_mm", "shared_add"))

        def loop(eng, front=None, back=None, send=None):
            def turn(b, q):
                for fn, w, p in ((front, b + 1, 1 - q), (back, b, q), (send, b - 1, 1 - q)):
                    if fn is not None and (not isinstance(w, int) or 0 <= w < B):
                        fn(w, p)
            if front is not None:
                front(0, 0)
            for b in range(2):
                turn(b, b)
            with eng.Fori(1, B // 2 - 1) as t:
                turn(t * 2, 0)
                turn(t * 2 + 1, 1)
            for b in range(B - 2, B + 1):
                turn(b, b % 2)

        def sent(q, b):
            return b // 2 * (16 * TJ * K) if isinstance(b, int) else (b - q) * (8 * TJ * K)

        @block.sync
        def _(sp):
            sp.dma_start(wr[:, :], wr_d).then_inc(loaded, 16)
            sp.dma_start(sgu[:, :, :, :], sgu_d).then_inc(loaded, 16)
            sp.dma_start(sd[:, :, :], sd_d).then_inc(loaded, 16)
            for e in range(0, NE, 16):
                sp.dma_start(gu[:, e:e + 16], gu_d[:, e:e + 16]).then_inc(gu_loaded, 16)
                sp.dma_start(down[:, e:e + 16], down_d[:, e:e + 16]).then_inc(gu_loaded, 16)
            plan_sp(sp)
            sp.wait_ge(gu_loaded, 16 * 2 * (NE // 16))

        @block.tensor
        def _(pe):
            def front(b, q):
                if isinstance(b, int) and b == 0:
                    pe.wait_ge(loaded, 48)
                    pe.wait_ge(made, 4)
                pe.wait_ge(h_taken, b + 1)
                need(pe, based, b)
                for j in range(TJ):
                    mm = nc.tensor.transpose(psT[:, j * P:(j + 1) * P], hcur[:, j * P:(j + 1) * P], ident[:, :])
                mm.then_inc(h_tok, 1)
                pe.wait_ge(norm, b + 1)
                need(pe, copied, b)
                for j in range(TJ):
                    mm = nc.tensor.transpose(psR[:, j * P:(j + 1) * P], xf[:, q, j, :], ident[:, :])
                mm.then_inc(back, 1)

            def rest(b, q):
                pe.wait_ge(copied, b + 1)
                need(pe, exped, b * TJ)
                for j in range(TJ):
                    mm = nc.tensor.matmul(psG[:, j * NE:(j + 1) * NE], xfT[:, q, j * P:(j + 1) * P], wr[:, :],
                                          start=True, stop=True)
                mm.then_inc(logits, 1)
                for s in range(NS):
                    need(pe, gated, b * NS + s)
                    nc.tensor.matmul(psA[:, :], sgu[:, s, 0, :], xfT[:, q, :], start=True, stop=True)\
                      .then_inc(gate_mm, 1)
                    need(pe, hidden, b * NS + s)
                    nc.tensor.matmul(psU[:, :], sgu[:, s, 1, :], xfT[:, q, :], start=True, stop=True)\
                      .then_inc(up_mm, 1)
                pe.wait_ge(hidden, b * NS + NS)
                need(pe, shared_add, b)
                for j in range(TJ):
                    for s in range(NS):
                        mm = nc.tensor.matmul(psY[:, j * P:(j + 1) * P], hs[:, s, j * P:(j + 1) * P], sd[:, s, :],
                                              start=(s == 0), stop=(s == NS - 1))
                mm.then_inc(shared_mm, 1)
                pe.wait_ge(taken, b + 1)
                need(pe, moved, b)
                for j in range(TJ):
                    for i in range(j):
                        nc.tensor.matmul(psK[:, j * NE:(j + 1) * NE], ones[:, :], took[:, i, :],
                                         start=(i == 0), stop=False)
                    nc.tensor.matmul(psK[:, j * NE:(j + 1) * NE], before[:, :], took[:, j, :],
                                     start=(j == 0), stop=True)
                for j in range(TJ):
                    mm = nc.tensor.matmul(psK[:, TJ * NE:(TJ + 1) * NE], ones[:, :], took[:, j, :],
                                          start=(j == 0), stop=(j == TJ - 1))
                mm.then_inc(ranked, 1)
            loop(pe, front, rest)
            plan_pe(pe)

        @block.scalar
        def _(act):
            def take(b):
                need(act, h_tok, b)
                nc.scalar.activation(hcur[:, :], hT[:, bass.ds(b * T, T)], ACT.Copy).then_inc(h_taken, 1)

            def front(b, q):
                take(b)
                act.wait_ge(back, b + 1)
                need(act, up_mm, (b - 1) * NS)
                nc.scalar.activation(xfT[:, q, :], psR[:, :], ACT.Copy).then_inc(copied, 1)

            def rest(b, q):
                act.wait_ge(norm, b + 1)
                need(act, scattered[q], sent(q, b))
                nc.scalar.activation(rows[:, q].rearrange("p j d -> p (j d)"),
                                     xf[:, q].rearrange("p j d -> p (j d)"), ACT.Copy).then_inc(rows_copied, 1)
                act.wait_ge(maxed, b + 1)
                need(act, prob, b)
                for j in range(TJ):
                    nc.scalar.activation(ex[:, j, :], psG[:, j * NE:(j + 1) * NE], ACT.Exp, bias=nmax[:, j:j + 1],
                                         accum_out=esum[:, j:j + 1]).then_inc(exped, 1)
                for s in range(NS):
                    act.wait_ge(gate_mm, b * NS + s + 1)
                    need(act, hidden, b * NS)
                    nc.scalar.activation(sg[:, s, :], psA[:, :], ACT.Silu).then_inc(gated, 1)
            loop(act, front, rest)
            plan_act(act)

        @block.gpsimd
        def _(pool):
            nc.gpsimd.memset(mhalf[:, :], -0.5).then_inc(cleared, 1)
            nc.gpsimd.memset(eps[:, :], EPS).then_inc(cleared, 1)
            nc.gpsimd.memset(ones[:, :], 1.0).then_inc(cleared, 1)
            nc.gpsimd.memset(before[:, :], 1.0).then_inc(cleared, 1)
            nc.gpsimd.iota(iota[:, :], [[1, NE]], base=0, channel_multiplier=0,
                           allow_small_or_imprecise_dtypes=True).then_inc(made, 1)
            nc.gpsimd.iota(base[:, :], [[REGION, NE]], base=0, channel_multiplier=0,
                           allow_small_or_imprecise_dtypes=True).then_inc(made, 1)
            plan_pool(pool)
            pool.wait_ge(cleared, 4)
            nc.gpsimd.affine_select(out=before[:, :], in_=before[:, :], compare_op=ALU.is_gt, fill=0.0, base=0,
                                    pattern=[[1, P]], channel_multiplier=-1).then_inc(made, 2)

            def scatter(b, q):
                need(pool, carried, b)
                pool.wait_ge(rows_copied, b + 1)
                pool.wait_ge(slotted, b + 1)
                nc.gpsimd.tensor_tensor(pspare[:, :], eps[0:1, 0:1], eps[0:1, 0:1], ALU.add).then_inc(carried, 1)
                for j in range(TJ):
                    for k in range(K):
                        c = j * K + k
                        nc.gpsimd.indirect_dma_start(
                            out=xs, out_offset=bass.IndirectOffsetOnAxis(ap=sli[:, q, c:c + 1], axis=0),
                            in_=rows[:, q, j, :], in_offset=None).then_inc(scattered[q], 16)

            def root(b, q):
                pool.wait_ge(aggr, b + 1)
                nc.gpsimd.tensor_tensor(ve[:, :], mv[:, :, 1], eps[:, :], ALU.add).then_inc(var_eps, 1)
                pool.wait_ge(var_eps, b + 1)
                nc.gpsimd.tensor_tensor(rs[:, :], ve[:, :], mhalf[:, :], ALU.pow).then_inc(rstd, 1)

            loop(pool, root, None, scatter)
            for q in range(2):
                pool.wait_ge(scattered[q], 16 * TJ * K * (B // 2))

        @block.vector
        def _(dve):
            def front(b, q):
                if isinstance(b, int) and b == 0:
                    dve.wait_ge(made, 4)
                dve.wait_ge(h_tok, b + 1)
                for j in range(TJ):
                    nc.vector.bn_stats(st[:, j, :], psT[:, j * P:(j + 1) * P]).then_inc(stats, 1)
                dve.wait_ge(stats, b * TJ + TJ)
                nc.vector.memset(spare[:, :], 0.0)
                for j in range(TJ):
                    ins = nc.vector.bn_aggr(mv[:, j, :], st[:, j, :])
                ins.then_inc(aggr, 1)
                need(dve, rows_copied, b - 1)
                need(dve, back, b - 1)
                dve.wait_ge(rstd, b + 1)
                for j in range(TJ):
                    ins = nc.vector.tensor_scalar(xf[:, q, j, :], psT[:, j * P:(j + 1) * P], mv[:, j, 0:1],
                                                  rs[:, j:j + 1], ALU.subtract, ALU.mult)
                ins.then_inc(norm, 1)
                dve.wait_ge(norm, b + 1)
                nc.vector.tensor_tensor(res[:, bass.ds(b * (TJ * D), TJ * D)], psT[:, :],
                                        xf[:, q].rearrange("p j d -> p (j d)"), ALU.add).then_inc(based, 1)

            def rest(b, q):
                dve.wait_ge(logits, b + 1)
                g3 = psG[:, 0:TJ * NE].rearrange("p (j e) -> p j e", j=TJ)
                nc.vector.tensor_reduce(nmax[:, :], g3, AX.X, ALU.max, negate=True).then_inc(maxed, 1)
                dve.wait_ge(exped, b * TJ + TJ)
                nc.vector.reciprocal(erec[:, :], esum[:, :]).then_inc(inv, 1)
                dve.wait_ge(inv, b + 1)
                nc.vector.tensor_tensor(probs[:, :, :], ex[:, :, :],
                                        erec[:, :].unsqueeze(2).to_broadcast([P, TJ, NE]), ALU.mult).then_inc(prob, 1)
                dve.wait_ge(prob, b + 1)
                nc.vector.memset(spare[:, :], 0.0)
                for j in range(TJ):
                    nc.vector.max(top[:, j, :], probs[:, j, :]).then_inc(topped, 1)
                dve.wait_ge(topped, b * TJ + TJ)
                nc.vector.memset(spare[:, :], 0.0)
                for j in range(TJ):
                    nc.vector.max_index(topi[:, j, :], top[:, j, :], probs[:, j, :]).then_inc(indexed, 1)
                nc.vector.tensor_reduce(tsum[:, :], top[:, :, 0:K], AX.X, ALU.add).then_inc(tsummed, 1)
                dve.wait_ge(indexed, b * TJ + TJ)
                nc.vector.tensor_copy(idxf[:, :, :], topi[:, :, 0:K]).then_inc(floated, 1)
                dve.wait_ge(tsummed, b + 1)
                nc.vector.reciprocal(trec[:, :], tsum[:, :]).then_inc(tinv, 1)
                dve.wait_ge(floated, b + 1)
                need(dve, kept, b)
                nc.vector.tensor_tensor(one[:, :, :],
                                        idxf[:, :, :].rearrange("p j k -> p (j k)").unsqueeze(2)
                                        .to_broadcast([P, TJ * K, NE]),
                                        iota[:, :].unsqueeze(1).to_broadcast([P, TJ * K, NE]),
                                        ALU.is_equal).then_inc(onehot, 1)
                dve.wait_ge(tinv, b + 1)
                nc.vector.tensor_tensor(wts[:, bass.ds(b * (TJ * K), TJ * K)].rearrange("p (j k) -> p j k", j=TJ),
                                        top[:, :, 0:K], trec[:, :].unsqueeze(2).to_broadcast([P, TJ, K]), ALU.mult)\
                  .then_inc(weighed, 1)
                dve.wait_ge(onehot, b + 1)
                need(dve, ranked, b)
                with nc.allow_low_precision("sums of at most six ones"):
                    nc.vector.tensor_reduce(took[:, :, :], one[:, :, :].rearrange("p (j k) e -> p j e k", j=TJ),
                                            AX.X, ALU.add).then_inc(taken, 1)
                nc.vector.tensor_copy(oh[:, bass.ds(b * (TJ * K * NE), TJ * K * NE)],
                                      one[:, :, :].rearrange("p c e -> p (c e)")).then_inc(kept, 1)
                for s in range(NS):
                    dve.wait_ge(up_mm, b * NS + s + 1)
                    dve.wait_ge(gated, b * NS + s + 1)
                    need(dve, shared_mm, b)
                    nc.vector.tensor_tensor(hs[:, s, :], psU[:, :], sg[:, s, :], ALU.mult).then_inc(hidden, 1)
                dve.wait_ge(ranked, b + 1)
                need(dve, moved, b)
                nc.vector.tensor_tensor(pos[:, :, :], psK[:, 0:TJ * NE].rearrange("p (j e) -> p j e", j=TJ),
                                        base[:, :].unsqueeze(1).to_broadcast([P, TJ, NE]), ALU.add).then_inc(placed, 1)
                dve.wait_ge(placed, b + 1)
                nc.vector.tensor_tensor(base[:, :], base[:, :], psK[:, TJ * NE:(TJ + 1) * NE], ALU.add)\
                  .then_inc(moved, 1)
                for j in range(TJ):
                    ins = nc.vector.tensor_tensor(tmp[:, j], one[:, j * K:(j + 1) * K, :],
                                                  pos[:, j, :].unsqueeze(1).to_broadcast([P, K, NE]), ALU.mult)
                ins.then_inc(masked, 1)
                dve.wait_ge(masked, b + 1)
                nc.vector.tensor_reduce(slf[:, :], tmp[:, :, :, :].rearrange("p j k e -> p (j k) e"), AX.X, ALU.add)\
                  .then_inc(summed, 1)
                dve.wait_ge(summed, b + 1)
                nc.vector.tensor_copy(slotx[:, bass.ds(b * (TJ * K), TJ * K)], slf[:, :])
                need(dve, scattered[q], sent(q, b))
                nc.vector.tensor_copy(sli[:, q, :], slf[:, :]).then_inc(slotted, 1)
                dve.wait_ge(shared_mm, b + 1)
                dve.wait_ge(based, b + 1)
                r = res[:, bass.ds(b * (TJ * D), TJ * D)]
                nc.vector.tensor_tensor(r, r, psY[:, :], ALU.add).then_inc(shared_add, 1)
            loop(dve, front, rest)
            dve.wait_ge(shared_add, B)
            plan_dve(dve)


def experts(nc, mem, sem, xs, ys):
    gu, down, ident, tile_e, tile_row = (mem[n] for n in ("gu", "down", "ident", "tile_e", "tile_row"))
    GR = 4
    NG = BLOCKS // GR
    ys_v = ys.rearrange("(g n p) d -> g p n d", n=GR, p=P)
    with ExitStack() as ctx:
        def sb(name, shape, dt=F32):
            return ctx.enter_context(nc.sbuf_tensor(name, shape, dt))

        def ps(name):
            return ctx.enter_context(nc.psum_tensor(name, [P, 512], F32))

        NX = 2
        xb = sb("e_rows", [P, NX, GR, D])
        xT = sb("e_rows_T", [P, 2, GR * P])
        sg = sb("e_silu", [P, 2, GR, F])
        hd = sb("e_hidden", [P, 2, GR, F])
        hTt = sb("e_hidden_T", [P, 2, GR * P])
        yb = sb("e_out", [P, 2, GR, D])
        psX, psH, psY = ps("ps_eX"), ps("ps_eH"), ps("ps_eY")
        psG = [ps(f"ps_eG{n}") for n in range(4)]
        block = ctx.enter_context(nc.Block())
        loaded = [sem(f"e_loaded{n}") for n in range(NX)]
        rows_T, rows_copied, gu_mm, silu, hidden = (sem("e_rows_T_ok"), sem("e_rows_copied"), sem("e_gu"),
                                                    sem("e_silu_ok"), sem("e_hidden_ok"))
        hid_T, hid_copied, down_mm, out_copied = (sem("e_hid_T"), sem("e_hid_copied"), sem("e_down"),
                                                  sem("e_out_copied"))
        stored = [sem(f"e_stored{n}") for n in range(2)]

        order = [(2, "a"), (3, "a"), (1, "a"), (2, "b"), (3, "b")]

        def pipeline(eng, **steps):
            def turn(g, q):
                for stage, step in order:
                    fn = steps.get(f"s{stage}{step}")
                    w = g - (stage - 1)
                    if fn is not None and (not isinstance(w, int) or 0 <= w < NG):
                        fn(w, (q + stage - 1) % 2)
            for g in range(4):
                turn(g, g % 2)
            with eng.Fori(2, NG // 2) as t:
                turn(t * 2, 0)
                turn(t * 2 + 1, 1)
            for g in range(NG, NG + 2):
                turn(g, g % 2)

        def read(engine, table, first, count, top):
            return nc.values_load_multi_w_load_instructions(table[0:1, bass.ds(first, count)], engines=(engine,),
                                                            min_val=0, max_val=top)[1]

        def experts_of(g):
            v = nc.tensor.value_load(tile_e[0:1, bass.ds(g, 1)], min_val=0, max_val=NE ** GR - 1)
            return [(v // NE ** n) % NE for n in range(GR)]

        def turns_of(g, q, n):
            return (g // 2 + 1) * n if isinstance(g, int) else (g - q) * (n // 2) + n

        @block.sync
        def _(sp):
            def load(g, q):
                need(sp, rows_T, g - 1)
                rows = read(mybir.EngineType.SP, tile_row, g * GR, GR, NE * REGION - P)
                for n in range(GR):
                    sp.dma_start(xb[:, q, n, :], xs[bass.ds(rows[n], P), :]).then_inc(loaded[q], 16)
            pipeline(sp, s1a=load)

        @block.gpsimd
        def _(pool):
            def store(g, q):
                pool.wait_ge(out_copied, g + 1)
                pool.dma_start(ys_v[bass.ds(g, 1)].rearrange("o p n d -> (o p) n d"), yb[:, q]).then_inc(stored[q], 16)
            pipeline(pool, s3b=store)
            for q in range(2):
                pool.wait_ge(stored[q], 16 * (NG // 2))

        @block.tensor
        def _(pe):
            def turn_rows(g, q):
                pe.wait_ge(loaded[q], turns_of(g, q, 16 * GR))
                need(pe, rows_copied, g)
                for n in range(GR):
                    mm = nc.tensor.transpose(psX[:, n * P:(n + 1) * P], xb[:, q, n, :], ident[:, :])
                mm.then_inc(rows_T, 1)

            def gate_up(m):
                def step(g, q):
                    es = experts_of(g)[2 * m:2 * m + 2]
                    if m == 0:
                        pe.wait_ge(rows_copied, g + 1)
                        need(pe, hidden, (g - 1) * 2)
                    for n in range(2):
                        mm = nc.tensor.matmul(psG[2 * q + m][:, n * 2 * F:(n + 1) * 2 * F],
                                              xT[:, q, (2 * m + n) * P:(2 * m + n + 1) * P],
                                              gu[:, bass.ds(es[n], 1), :, :].rearrange("p o a f -> p (o a f)"),
                                              start=True, stop=True)
                    mm.then_inc(gu_mm, 1)
                return step

            def turn_hidden(g, q):
                pe.wait_ge(hidden, g * 2 + 2)
                need(pe, hid_copied, g)
                for n in range(GR):
                    mm = nc.tensor.transpose(psH[:, n * P:(n + 1) * P], hd[:, q, n, :], ident[:, :])
                mm.then_inc(hid_T, 1)

            def out_rows(g, q):
                es = experts_of(g)
                pe.wait_ge(hid_copied, g + 1)
                need(pe, out_copied, g)
                for n in range(GR):
                    mm = nc.tensor.matmul(psY[:, n * P:(n + 1) * P], hTt[:, q, n * P:(n + 1) * P],
                                          down[:, bass.ds(es[n], 1), :].rearrange("p o d -> p (o d)"),
                                          start=True, stop=True)
                mm.then_inc(down_mm, 1)
            pipeline(pe, s1a=turn_rows, s2a=gate_up(0), s2b=gate_up(1), s3a=turn_hidden, s3b=out_rows)

        @block.scalar
        def _(act):
            def copy_rows(g, q):
                act.wait_ge(rows_T, g + 1)
                need(act, gu_mm, (g - 1) * 2)
                nc.scalar.activation(xT[:, q, :], psX[:, :], ACT.Copy).then_inc(rows_copied, 1)

            def gate(m):
                def step(g, q):
                    act.wait_ge(gu_mm, g * 2 + m + 1)
                    need(act, hidden, (g - 1) * 2)
                    nc.scalar.activation(sg[:, q, 2 * m:2 * m + 2, :],
                                         psG[2 * q + m][:, :].rearrange("p (n a f) -> p n a f", n=2, a=2)[:, :, 0, :],
                                         ACT.Silu).then_inc(silu, 1)
                return step

            def copy_out(g, q):
                act.wait_ge(down_mm, g + 1)
                if not isinstance(g, int) or g >= 2:
                    act.wait_ge(stored[q], turns_of(g, q, 16) - 16)
                nc.scalar.activation(yb[:, q].rearrange("p n d -> p (n d)"), psY[:, :], ACT.Copy)\
                  .then_inc(out_copied, 1)
            pipeline(act, s1a=copy_rows, s2a=gate(0), s2b=gate(1), s3b=copy_out)

        @block.vector
        def _(dve):
            def multiply(m):
                def step(g, q):
                    dve.wait_ge(silu, g * 2 + m + 1)
                    need(dve, hid_T, g - 1)
                    nc.vector.tensor_tensor(hd[:, q, 2 * m:2 * m + 2, :], sg[:, q, 2 * m:2 * m + 2, :],
                                            psG[2 * q + m][:, :].rearrange("p (n a f) -> p n a f", n=2, a=2)[:, :, 1, :],
                                            ALU.mult).then_inc(hidden, 1)
                return step

            def copy_hidden(g, q):
                dve.wait_ge(hid_T, g + 1)
                need(dve, down_mm, g - 1)
                nc.vector.tensor_copy(hTt[:, q, :], psH[:, :]).then_inc(hid_copied, 1)
            pipeline(dve, s2a=multiply(0), s2b=multiply(1), s3a=copy_hidden)


def combine(nc, mem, sem, ys, out):
    res, wts, sloty, ident = mem["res"], mem["wts"], mem["sloty"], mem["ident"]
    out_v = out.rearrange("b t d -> (b t) d").rearrange("(n p) d -> n p d", p=P)
    with ExitStack() as ctx:
        NB = 4
        idx = ctx.enter_context(nc.sbuf_tensor("c_index", [P, NB, K], I32))
        yg = ctx.enter_context(nc.sbuf_tensor("c_rows", [P, NB, K, D], F32))
        acc = ctx.enter_context(nc.sbuf_tensor("c_acc", [P, NB, D], F32))
        w = ctx.enter_context(nc.sbuf_tensor("c_weights", [P, NB, K], F32))
        spare = ctx.enter_context(nc.sbuf_tensor("c_spare", [1, 1], F32))
        block = ctx.enter_context(nc.Block())
        indexed, added, done, wcopied = sem("c_indexed"), sem("c_added"), sem("c_done"), sem("c_wcopied")
        carried = sem("c_carried")
        fetched = [sem(f"c_fetched{n}") for n in range(NB)]
        stored = [sem(f"c_stored{n}") for n in range(NB)]

        def loop(eng, body):
            for n in range(NB):
                body(n, n)
            with eng.Fori(1, TILES // NB) as t:
                for n in range(NB):
                    body(t * NB + n, n)

        @block.scalar
        def _(act):
            def body(t, n):
                if isinstance(t, int):
                    pass
                else:
                    act.wait_ge(fetched[n], (t - n) * (16 * K // NB))
                nc.scalar.activation(idx[:, n, :], sloty[:, bass.ds(t * K, K)], ACT.Copy).then_inc(indexed, 1)
                need(act, done, t - (NB - 1))
                nc.scalar.activation(w[:, n, :], wts[:, bass.ds(t * K, K)], ACT.Copy).then_inc(wcopied, 1)
            loop(act, body)

        @block.gpsimd
        def _(pool):
            def body(t, n):
                need(pool, carried, t)
                pool.wait_ge(indexed, t + 1)
                need(pool, done, t - (NB - 1))
                nc.gpsimd.tensor_tensor(spare[:, :], ident[0:1, 0:1], ident[0:1, 0:1], ALU.add)\
                  .then_inc(carried, 1)
                for k in range(K):
                    nc.gpsimd.indirect_dma_start(
                        out=yg[:, n, k, :], out_offset=None, in_=ys,
                        in_offset=bass.IndirectOffsetOnAxis(ap=idx[:, n, k:k + 1], axis=0)).then_inc(fetched[n], 16)
            loop(pool, body)

        @block.vector
        def _(dve):
            def body(t, n):
                dve.wait_ge(wcopied, t + 1)
                if isinstance(t, int):
                    dve.wait_ge(fetched[n], 16 * K)
                else:
                    dve.wait_ge(stored[n], (t - n) * (16 // NB))
                    dve.wait_ge(fetched[n], (t - n) * (16 * K // NB) + 16 * K)
                for k in range(K):
                    src = res[:, bass.ds(t * D, D)] if k == 0 else acc[:, n, :]
                    if k:
                        dve.wait_ge(added, t * (K - 1) + k)
                    ins = nc.vector.scalar_tensor_tensor(out=acc[:, n, :], in0=yg[:, n, k, :], scalar=w[:, n, k:k + 1],
                                                         in1=src, op0=ALU.mult, op1=ALU.add)
                    ins.then_inc(added if k < K - 1 else done, 1)
            loop(dve, body)

        @block.sync
        def _(sp):
            def body(t, n):
                sp.wait_ge(done, t + 1)
                dst = out_v[bass.ds(t, 1)].rearrange("o p d -> (o p) d")
                sp.dma_start(dst, acc[:, n, :]).then_inc(stored[n], 16)
            loop(sp, body)
            for n in range(NB):
                sp.wait_ge(stored[n], 16 * (TILES // NB))


def build(nc, x, tok_wT, par_d, proj_w, out_w, cosT, sinT, wr, shared_gu, shared_d, gu, down, out):
    with ExitStack() as ctx:
        def sb(name, shape, dt=F32):
            return ctx.enter_context(nc.sbuf_tensor(name, shape, dt))

        n_sems = [0]

        def sem(name):
            n_sems[0] += 1
            return ctx.enter_context(nc.semaphore(name))

        mem = {
            "hT": sb("hT", [P, N]),
            "ident": sb("ident", [P, P]),
            "par": sb("par", [P, NPAR]),
            "tok_wT": sb("tok_wT_sb", [P, P]),
        }
        with nc.Block() as block:
            consts, zeroed = sem("consts_loaded"), sem("ident_zeroed")
            made = sem("ident_made")

            @block.sync
            def _(sp):
                sp.dma_start(mem["tok_wT"][:, :], tok_wT).then_inc(consts, 16)
                sp.dma_start(mem["par"][:, :], par_d).then_inc(consts, 16)
                sp.wait_ge(consts, 32)

            @block.gpsimd
            def _(pool):
                nc.gpsimd.memset(mem["ident"][:, :], 0.0).then_inc(zeroed, 1)
                pool.wait_ge(zeroed, 1)
                nc.gpsimd.affine_select(out=mem["ident"][:, :], in_=mem["ident"][:, :], compare_op=ALU.not_equal,
                                        fill=1.0, base=0, pattern=[[-1, P]], channel_multiplier=1).then_inc(made, 1)
                pool.wait_ge(made, 1)
        pool_chunks(nc, mem, sem, x, mem["tok_wT"])
        if STOP == "tok":
            return
        attention(nc, mem, sem, proj_w, out_w, cosT, sinT)
        if STOP == "attn":
            return
        xs = nc.dram_tensor("xs", (NE * REGION, D), F32, kind="Internal").ap()
        ys = nc.dram_tensor("ys", (BLOCKS * P, D), F32, kind="Internal").ap()
        mem |= {
            "res": sb("res", [P, TILES * D]),
            "wts": sb("wts", [P, TILES * K]),
            "slotx": sb("slotx", [P, TILES * K]),
            "sloty": sb("sloty", [P, TILES * K]),
            "oh": sb("onehots", [P, TILES * K * NE], BF16),
            "base": sb("next_row", [P, NE]),
            "gu": sb("gu_sb", [P, NE, 2, F]),
            "down": sb("down_sb", [P, NE, D]),
            "tile_e": sb("tile_e", [1, BLOCKS // 4], I32),
            "tile_row": sb("tile_row", [1, BLOCKS], I32),
        }
        route(nc, mem, sem, wr, shared_gu, shared_d, gu, down, xs)
        if STOP == "route":
            return
        experts(nc, mem, sem, xs, ys)
        combine(nc, mem, sem, ys, out)


STOP = ""


def kernel(**inputs):
    import numpy as _np
    import concourse.bacc as _bacc
    from concourse import mybir as _mybir
    from concourse.bass_utils import run_bass_kernel_spmd as _run

    a = {k: _np.asarray(v) for k, v in inputs.items()}
    L = "L0_attn_"

    def halves(v):
        return v.reshape(2, P).T

    swap = _np.arange(P) ^ 1
    cw = {n: a[L + n + "_cw"] for n in ("u", "v", "qk")}
    cols = [a["L0_tok_b"][:, None]]
    cols += [a[L + n + "_ln_g"][:, None] for n in ("u", "v", "qk")]
    cols += [a[L + n + "_ln_b"][:, None] for n in ("u", "v", "qk")]
    cols += [halves(a[L + "u_b"]), halves(a[L + "v_b"]), a[L + "qk_b"][:, None]]
    for t in range(3):
        cols += [halves(cw["u"][:, t]), halves(cw["v"][:, t]), cw["qk"][:, t:t + 1]]
    cols += [halves(a[L + "u_cb"]), halves(a[L + "v_cb"]), a[L + "qk_cb"][:, None]]
    cols += [halves(a[L + "out_ln_g"]), halves(a[L + "out_ln_b"]), a[L + "out_b"][:, None]]
    cols += [a[L + "out_cw"], a[L + "out_cb"][:, None]]
    cols += [a[L + "gamma"].T, a[L + "beta"].T, a[L + "gamma"].T[swap], a[L + "beta"].T[swap]]
    inv = (1.0 / 10000.0 ** (_np.arange(0, D, 2, dtype=_np.float32) / _np.float32(D))).astype(_np.float32)
    ang = _np.repeat(_np.arange(T, dtype=_np.float32)[:, None] * inv, 2, axis=-1)
    sign = _np.where(_np.arange(D) % 2 == 0, -1.0, 1.0).astype(_np.float32)[:, None]
    laid = {
        "x": a["x"],
        "tok_wT": a["L0_tok_W"].T,
        "par": _np.concatenate(cols, axis=1),
        "proj_w": _np.concatenate([a[L + "u_w"], a[L + "v_w"], a[L + "qk_w"]], axis=1),
        "out_w": a[L + "out_w"].reshape(2, P, P).transpose(1, 0, 2),
        "cosT": _np.cos(ang).T.astype(_np.float32),
        "sinT": _np.sin(ang).T.astype(_np.float32) * sign,
        "wr": a["L0_ffn_Wr"],
        "shared_gu": _np.stack([a["L0_ffn_sWg"], a["L0_ffn_sWu"]], axis=2).transpose(1, 0, 2, 3),
        "shared_d": a["L0_ffn_sWd"].transpose(1, 0, 2),
        "gu": _np.stack([a["L0_ffn_Wg"], a["L0_ffn_Wu"]], axis=2).transpose(1, 0, 2, 3),
        "down": a["L0_ffn_Wd"].transpose(1, 0, 2),
    }
    nc = _bacc.Bacc("TRN2", target_bir_lowering=False, num_devices=1)
    arrays, args = {}, []
    for name, v in laid.items():
        v = _np.ascontiguousarray(v)
        arrays[f"in_{name}"] = v
        args.append(nc.dram_tensor(f"in_{name}", v.shape, _mybir.dt.from_np(v.dtype), kind="ExternalInput").ap())
    args.append(nc.dram_tensor("out_h", (B, T, D), F32, kind="ExternalOutput").ap())
    build(nc, *args)
    r = _run(nc, [arrays], core_ids=[0])
    return r.results[0]["out_h"]
```

```python
import math

import numpy as np

import concourse.bass as bass
from concourse import mybir
from contextlib import ExitStack

F32 = mybir.dt.float32
BF16 = mybir.dt.bfloat16
U32 = mybir.dt.uint32
I32 = mybir.dt.int32
ALU = mybir.AluOpType
ACT = mybir.ActivationFunctionType
AX = mybir.AxisListType

P = 128
B, S, D = 8, 8192, 128
CHUNK = 16
T = S // CHUNK
N = B * T
H = 256
G = 64
NE, NS, K = 64, 2, 6
F = 128
TJ = T // P
EPS = 1e-5

PAR = {}
_at = 0
for _name, _n in (("tok_b", 1), ("ln_g", 3), ("ln_b", 3), ("proj_b", 5), ("cw0", 5), ("cw1", 5), ("cw2", 5),
                  ("cb", 5), ("out_g", 2), ("out_lb", 2), ("out_b", 1), ("out_cw", 3), ("out_cb", 1),
                  ("gamma", 4), ("beta", 4), ("gamma_sw", 4), ("beta_sw", 4)):
    PAR[_name] = _at
    _at += _n
NPAR = _at


def need(eng, semaphore, value):
    if not isinstance(value, int) or value > 0:
        eng.wait_ge(semaphore, value)


def pool_chunks(nc, mem, sem, x_dram, later, later_loaded):
    SUPER, UNITS = 2048, 4
    NSUPER = B * S // SUPER
    A, GU = 4, 32
    hT, ident, par, wT = mem["hT"], mem["ident"], mem["par"], mem["tok_wT"]
    x_v = x_dram.rearrange("b s d -> (b s) d").rearrange("(n u p a) d -> n p u (a d)", u=UNITS, p=P, a=A)

    with ExitStack() as ctx:
        def sb(name, shape, dt=F32):
            return ctx.enter_context(nc.sbuf_tensor(name, shape, dt))

        R = 4
        xin = sb("x_in", [P, 2, UNITS, A * D])
        xT = sb("x_T", [P, 2 * R, 512])
        minus = sb("x_minus", [P, P])
        shifted = sb("x_shift", [P, 512])
        ex = sb("x_exp", [P, R, 512])
        xe = sb("x_weighted", [P, R, 512])
        eh = sb("x_exp_halves", [P, R, GU, CHUNK // 2])
        mx = sb("x_max", [P, 2, GU])
        mb = sb("x_max_bias", [P, R, GU])
        esum = sb("x_esum", [P, 2, UNITS, GU])
        wsum = sb("x_wsum", [P, 2, UNITS, GU])
        rec = sb("x_rec", [P, 2, UNITS, GU])
        psX = [ctx.enter_context(nc.psum_tensor(f"ps_xT{i}", [P, 512], F32)) for i in range(2)]
        psL = [ctx.enter_context(nc.psum_tensor(f"ps_logit{i}", [P, 512], F32)) for i in range(R)]
        block = ctx.enter_context(nc.Block())
        b_tok = par[:, PAR["tok_b"]:PAR["tok_b"] + 1]

        loaded = [sem(f"x_loaded{i}") for i in range(2)]
        transposed, copied, logits = sem("x_transposed"), sem("x_copied"), sem("x_logits")
        maxed, biased, subtracted, exped = sem("x_maxed"), sem("x_biased"), sem("x_subtracted"), sem("x_exped")
        weighted, esummed, wsummed = sem("x_weighted_ok"), sem("x_esummed"), sem("x_wsummed")
        minus_made = sem("x_minus_made")
        subtracted_pe = sem("x_subtracted_pe")
        ehalved, inverted, pooled = sem("x_ehalved"), sem("x_inverted"), sem("x_pooled")
        LAST = NSUPER * UNITS - 1
        POOL_HALVES = (0, 1, 2)
        ON_PE = (0, 2, 3)

        def counted(units, u, v):
            k = v % UNITS
            return (u - k) * len(units) + UNITS * sum(w <= k for w in units)

        def subtracted_by(u, v):
            if v % UNITS in ON_PE:
                return subtracted_pe, counted(ON_PE, u, v)
            return subtracted, counted([w for w in range(UNITS) if w not in ON_PE], u, v)

        def wait_subtracted(eng, u, v):
            if not isinstance(u, int) or u >= 0:
                eng.wait_ge(*subtracted_by(u, v % UNITS))

        def pipeline(eng, lag, steps):
            def turn(u, v):
                for lag, step in steps:
                    w = u - lag
                    if not isinstance(u, int) or 0 <= w <= LAST:
                        step(w, (v - lag) % (2 * UNITS))
            for u in range(4 * UNITS):
                turn(u, u % (2 * UNITS))
            with eng.Fori(2, NSUPER // 2) as i:
                for v in range(2 * UNITS):
                    turn(i * (2 * UNITS) + v, v)
            for u in range(LAST + 1, LAST + 1 + lag):
                turn(u, u % (2 * UNITS))

        @block.sync
        def _(sp):
            for n in range(2):
                sp.dma_start(xin[:, n], x_v[n]).then_inc(loaded[n], 16)
            for dst, src in later:
                sp.dma_start(dst[:], src).then_inc(later_loaded, 16)
            with sp.Fori(1, NSUPER // 2) as i:
                for n in range(2):
                    sp.wait_ge(transposed, (i * 2 + n - 1) * UNITS)
                    sp.dma_start(xin[:, n], x_v[bass.ds(i * 2 + n, 1)].rearrange("o p u k -> (o p) u k"))\
                      .then_inc(loaded[n], 16)

        @block.tensor
        def _(pe):
            pe.wait_ge(minus_made, 1)
            def transposes(u, v):
                n, k = v // UNITS, v % UNITS
                if k == 0:
                    if isinstance(u, int):
                        pe.wait_ge(loaded[n], 16 * (u // (2 * UNITS) + 1))
                    else:
                        pe.wait_ge(loaded[n], (u - v) * (16 // (2 * UNITS)) + 16)
                need(pe, copied, u - 1)
                for a in range(A):
                    mm = nc.tensor.transpose(psX[v % 2][:, a * P:(a + 1) * P],
                                             xin[:, n, k, a * D:(a + 1) * D], ident[:, :])
                mm.then_inc(transposed, 1)

            def project(u, v):
                pe.wait_ge(copied, u + 1)
                need(pe, exped, u - (R - 1))
                nc.tensor.matmul(psL[v % R][:, :], wT[:, :], xT[:, v, :], start=True, stop=True)\
                  .then_inc(logits, 1)

            def subtract(u, v):
                if v % UNITS not in ON_PE:
                    return
                pe.wait_ge(biased, u + 1)
                nc.tensor.matmul(psL[v % R][:, :].rearrange("d (g c) -> d g c", g=GU), minus[:, :],
                                 mb[:, v % R, :].unsqueeze(2).to_broadcast([P, GU, CHUNK]), start=False, stop=True,
                                 skip_group_check=True).then_inc(subtracted_pe, UNITS)
            pipeline(pe, 3, ((0, transposes), (3, subtract), (1, project)))

        @block.scalar
        def _(act):
            def copy(u, v):
                act.wait_ge(transposed, u + 1)
                need(act, weighted, u - (2 * R - 1))
                nc.scalar.activation(xT[:, v, :].rearrange("d (g a q) -> d a g q", g=GU, a=A),
                                     psX[v % 2][:, :].rearrange("d (a g q) -> d a g q", a=A, g=GU),
                                     ACT.Copy).then_inc(copied, 1)

            def add_bias(u, v):
                act.wait_ge(maxed, u + 1)
                wait_subtracted(act, u - R, v)
                nc.scalar.activation(mb[:, v % R, :], mx[:, v % 2, :], ACT.Identity, bias=b_tok).then_inc(biased, 1)

            def exp(u, v):
                wait_subtracted(act, u, v)
                need(act, weighted, u - (R - 1))
                if not isinstance(u, int) or u >= R:
                    if v % UNITS in POOL_HALVES:
                        act.wait_ge(ehalved, counted(POOL_HALVES, u - R, v))
                    else:
                        act.wait_ge(esummed, u - R + 1)
                src = psL[v % R] if v % UNITS in ON_PE else shifted
                nc.scalar.activation(ex[:, v % R, :], src[:, :], ACT.Exp, bias=b_tok).then_inc(exped, 1)
            pipeline(act, 4, ((0, copy), (2, add_bias), (4, exp)))

        @block.gpsimd
        def _(pool):
            def weigh(u, v):
                pool.wait_ge(exped, u + 1)
                need(pool, wsummed, u - (R - 1))
                nc.gpsimd.tensor_tensor(xe[:, v % R, :], xT[:, v, :], ex[:, v % R, :], ALU.mult)\
                  .then_inc(weighted, 1)
                if v % UNITS in POOL_HALVES:
                    need(pool, esummed, u - (R - 1))
                    e3 = ex[:, v % R, :].rearrange("d (g c) -> d g c", g=GU)
                    nc.gpsimd.tensor_tensor(eh[:, v % R], e3[:, :, 0:CHUNK // 2], e3[:, :, CHUNK // 2:], ALU.add)\
                      .then_inc(ehalved, UNITS)

            def scale(u, v):
                if v % UNITS != UNITS - 1:
                    return
                n = v // UNITS
                pool.wait_ge(inverted, u + 1)
                nc.gpsimd.tensor_tensor(hT[:, bass.ds((u - (UNITS - 1)) * GU, UNITS * GU)],
                                        wsum[:, n].rearrange("d u g -> d (u g)"),
                                        rec[:, n].rearrange("d u g -> d (u g)"), ALU.mult).then_inc(pooled, UNITS)
            pipeline(pool, 7, ((4, weigh), (7, scale)))
            pool.wait_ge(pooled, LAST + 1)

        @block.vector
        def _(dve):
            def maximum(u, v):
                dve.wait_ge(logits, u + 1)
                need(dve, biased, u - 1)
                nc.vector.tensor_reduce(mx[:, v % 2, :], psL[v % R][:, :].rearrange("d (g c) -> d g c", g=GU),
                                        AX.X, ALU.max).then_inc(maxed, 1)

            def subtract(u, v):
                if v % UNITS in ON_PE:
                    return
                dve.wait_ge(biased, u + 1)
                need(dve, exped, u - (UNITS // (UNITS - len(ON_PE)) - 1))
                nc.vector.tensor_tensor(shifted[:, :].rearrange("d (g c) -> d g c", g=GU),
                                        psL[v % R][:, :].rearrange("d (g c) -> d g c", g=GU),
                                        mb[:, v % R, :].unsqueeze(2).to_broadcast([P, GU, CHUNK]),
                                        ALU.subtract).then_inc(subtracted, UNITS)

            def sums(u, v):
                n, k = v // UNITS, v % UNITS
                if k in POOL_HALVES:
                    dve.wait_ge(ehalved, counted(POOL_HALVES, u, v))
                    src = eh[:, v % R]
                else:
                    dve.wait_ge(exped, u + 1)
                    src = ex[:, v % R, :].rearrange("d (g c) -> d g c", g=GU)
                if k == 0:
                    need(dve, pooled, u - v % UNITS - UNITS)
                nc.vector.tensor_reduce(esum[:, n, k, :], src, AX.X, ALU.add).then_inc(esummed, 1)
                dve.wait_ge(weighted, u + 1)
                src = xe[:, v % R, :].rearrange("d (g c) -> d g c", g=GU)
                nc.vector.tensor_reduce(wsum[:, n, k, :], src, AX.X, ALU.add).then_inc(wsummed, 1)


            def invert(u, v):
                if v % UNITS != UNITS - 1:
                    return
                n = v // UNITS
                dve.wait_ge(wsummed, u + 1)
                need(dve, pooled, u - v % UNITS - UNITS)
                nc.vector.reciprocal(rec[:, n], esum[:, n]).then_inc(inverted, UNITS)
            nc.vector.tensor_scalar(minus[:, :], ident[:, :], -1.0, None, ALU.mult).then_inc(minus_made, 1)
            pipeline(dve, 7, ((6, sums), (1, maximum), (3, subtract), (7, invert)))


TILES = N // P
REGION = N + P
BLOCKS = -(-(-(-(N * K + NE * (P - 1)) // P)) // 4) * 4
ROW = D + 2 * K
PLACE0 = BLOCKS * P


def plan(nc, mem, sem, ctx, xs, psP):
    base, ident, iota = mem["base"], mem["ident"], mem["iota"]
    tile_e, tile_row, tile_eb, nowhere = (mem[n] for n in ("tile_e", "tile_row", "tile_eb", "nowhere"))
    HB = BLOCKS // P

    def sb(name, shape, dt=F32):
        return ctx.enter_context(nc.sbuf_tensor(name, shape, dt))

    region = sb("p_region", [P, NE])
    cnt = sb("p_count", [P, NE])
    cnti = sb("p_count_int", [P, NE], I32)
    msk = sb("p_masked_int", [P, NE], I32)
    padded = sb("p_padded", [P, NE])
    ends, starts, shift = sb("p_ends", [P, NE]), sb("p_starts", [P, NE]), sb("p_shift", [P, NE])
    zero_e = sb("p_zero_e", [P, NE])
    first = sb("p_first", [P, HB])
    cmp = sb("p_cmp", [P, HB, NE])
    te, tr, valid, sh = (sb("p_" + n, [P, HB]) for n in ("te", "tr", "valid", "sh"))
    tails = sb("p_tails", [1, NE], I32)
    zeros = sb("p_zeros", [P, ROW])
    teb = sb("p_te_bcast", [P, HB, P])
    er = sb("p_te_row", [1, BLOCKS])
    pk = sb("p_packed", [1, BLOCKS // 4])
    made, chain, turned, tails_ok, tailed = (sem("p_made"), sem("p_step"), sem("p_turned"), sem("p_tails_ok"),
                                             sem("p_tailed"))
    cols = sem("p_cols_ok")
    spread = sem("p_spread")

    def on_pool(pool):
        nc.gpsimd.iota(region[:, :], [[REGION, NE]], base=0, channel_multiplier=0,
                       allow_small_or_imprecise_dtypes=True).then_inc(made, 1)
        nc.gpsimd.iota(first[:, :], [[P * P, HB]], base=0, channel_multiplier=P,
                       allow_small_or_imprecise_dtypes=True).then_inc(made, 1)
        nc.gpsimd.memset(zero_e[:, :], 0.0).then_inc(made, 1)
        nc.gpsimd.memset(zeros[:, 0:D], 0.0).then_inc(made, 1)
        nc.gpsimd.memset(zeros[:, D:ROW], -1.0).then_inc(made, 1)
        nc.gpsimd.iota(nowhere[:, :], [[P, BLOCKS]], base=0, channel_multiplier=1,
                       allow_small_or_imprecise_dtypes=True).then_inc(made, 1)

    def on_dve(dve):
        n = [0]

        def step(ins):
            n[0] += 1
            ins.then_inc(chain, 1)
            dve.wait_ge(chain, n[0])

        dve.wait_ge(made, 6)
        nc.vector.tensor_copy(tails[0:1, :], base[0:1, :]).then_inc(tails_ok, 1)
        step(nc.vector.tensor_tensor(cnt[:, :], base[:, :], region[:, :], ALU.subtract))
        step(nc.vector.tensor_scalar(cnt[:, :], cnt[:, :], float(P - 1), None, ALU.add))
        step(nc.vector.tensor_copy(cnti[:, :], cnt[:, :]))
        step(nc.vector.tensor_scalar(msk[:, :], cnti[:, :], -P, None, ALU.bitwise_and))
        step(nc.vector.tensor_copy(padded[:, :], msk[:, :]))
        step(nc.vector.tensor_tensor_scan(ends[:, :], padded[:, :], zero_e[:, :], 0.0, ALU.add, ALU.add))
        step(nc.vector.tensor_tensor(starts[:, :], ends[:, :], padded[:, :], ALU.subtract))
        step(nc.vector.tensor_tensor(shift[:, :], starts[:, :], region[:, :], ALU.subtract))
        f3 = first[:, :].unsqueeze(2).to_broadcast([P, HB, NE])
        step(nc.vector.tensor_tensor(cmp[:, :, :], ends[:, :].unsqueeze(1).to_broadcast([P, HB, NE]), f3,
                                     ALU.is_le))
        step(nc.vector.tensor_reduce(te[:, :], cmp[:, :, :], AX.X, ALU.add))
        step(nc.vector.tensor_copy(teb[:, :, :], te[:, :].unsqueeze(2).to_broadcast([P, HB, P])))
        step(nc.vector.tensor_scalar(valid[:, :], te[:, :], float(NE), None, ALU.is_lt))
        step(nc.vector.tensor_scalar(te[:, :], te[:, :], float(NE - 1), None, ALU.min))
        step(nc.vector.tensor_tensor(cmp[:, :, :], iota[:, :].unsqueeze(1).to_broadcast([P, HB, NE]),
                                     te[:, :].unsqueeze(2).to_broadcast([P, HB, NE]), ALU.is_equal))
        step(nc.vector.tensor_tensor(cmp[:, :, :], cmp[:, :, :],
                                     shift[:, :].unsqueeze(1).to_broadcast([P, HB, NE]), ALU.mult))
        step(nc.vector.tensor_reduce(sh[:, :], cmp[:, :, :], AX.X, ALU.add))
        step(nc.vector.tensor_tensor(tr[:, :], first[:, :], sh[:, :], ALU.subtract))
        nc.vector.tensor_tensor(tr[:, :], tr[:, :], valid[:, :], ALU.mult).then_inc(cols, 1)
        dve.wait_ge(turned, 1)
        nc.vector.tensor_copy(tile_eb[:, :], psP[:, 0:BLOCKS]).then_inc(spread, 1)
        step(nc.vector.tensor_scalar(er[0:1, :], psP[0:1, 0:BLOCKS], float(NE - 1), None, ALU.min))
        e4 = er[0:1, :].rearrange("o (g n) -> o g n", n=4)
        step(nc.vector.tensor_copy(pk[0:1, :], e4[:, :, 3]))
        for m in (2, 1, 0):
            step(nc.vector.scalar_tensor_tensor(out=pk[0:1, :], in0=pk[0:1, :], scalar=float(NE), in1=e4[:, :, m],
                                                op0=ALU.mult, op1=ALU.add))
        nc.vector.tensor_copy(tile_e[0:1, :], pk[0:1, :])
        step(nc.vector.tensor_copy(tile_row[0:1, :], psP[0:1, BLOCKS:2 * BLOCKS]))
        dve.wait_ge(spread, 1)

    def on_pe(pe):
        pe.wait_ge(cols, 1)
        for h in range(HB):
            nc.tensor.matmul(psP[:, h * P:(h + 1) * P], teb[:, h, :], ident[:, :], start=True, stop=True)
        for h in range(HB):
            mm = nc.tensor.matmul(psP[0:1, BLOCKS + h * P:BLOCKS + (h + 1) * P], tr[:, h:h + 1],
                                  ident[:, :], start=True, stop=True)
        mm.then_inc(turned, 1)

    def clear_tails(eng, engine, first):
        eng.wait_ge(tails_ok, 1)
        eng.wait_ge(made, 6)
        with eng.Fori(0, NE // 2 // 4) as t:
            rows = nc.values_load_multi_w_load_instructions(
                tails[0:1, bass.ds(t * 4 + first, 4)], engines=(engine,), min_val=0, max_val=NE * REGION - P)[1]
            for row in rows:
                eng.dma_start(xs[bass.ds(row, P), :], zeros[:, :]).then_inc(tailed, 16)

    def on_sp(sp):
        clear_tails(sp, mybir.EngineType.SP, 0)
        sp.wait_ge(tailed, 16 * NE)

    def on_act(act):
        clear_tails(act, mybir.EngineType.Activation, NE // 2)

    return on_pool, on_dve, on_pe, on_sp, on_act


def batch_pipeline(eng, stages, order):
    def turn(i, parity):
        for stage, step in order:
            b = i - (stage - 1)
            if isinstance(b, int) and not 0 <= b < B:
                continue
            fn = stages.get(stage, {}).get(step[0])
            if fn is not None:
                fn(b, (parity + stage - 1) % 2, *([int(step[1:])] if step[1:] else []))

    for i in range(6):
        turn(i, i % 2)
    with eng.Fori(3, B // 2) as t:
        turn(t * 2, 0)
        turn(t * 2 + 1, 1)
    for i in range(B, B + 4):
        turn(i, i % 2)


def upto(b, ahead):
    return min(b + ahead + 1, B) if isinstance(b, int) else b + (ahead + 1)


def before_in_turn(one, other):
    return int(ORDER.index(one) < ORDER.index(other))


SENDS = 24
ORDER = [
    (1, "a"), (5, "e0"), (5, "e1"), (5, "e2"), (5, "e3"), (1, "n"), (2, "a0"), (5, "e4"), (2, "a1"),
    (2, "a2"), (5, "e5"), (4, "a"), (2, "a3"), (2, "a4"), (4, "n"), (5, "e6"), (2, "b0"), (2, "b1"),
    (5, "e7"), (5, "e8"), (3, "a"), (4, "b"), (5, "e9"), (5, "e10"), (5, "e11"), (4, "c"), (5, "e12"),
    (5, "e13"), (4, "g"), (2, "b2"), (2, "b3"), (5, "e14"), (5, "e15"), (3, "b0"), (5, "e16"), (3, "b1"),
    (2, "b4"), (5, "e17"), (5, "e18"), (4, "d"), (5, "e19"), (3, "c"), (4, "f"), (3, "n"), (5, "e20"),
    (5, "e21"), (5, "e22"), (5, "e23"), (1, "b"), (1, "m"), (3, "d"), (1, "c"), (4, "s"), (4, "t")
]

U0, V0, LK = 0, 2, 4
QQ, LQ, QK, KL = range(4)


def attend_and_route(nc, mem, sem, w_loaded, gu_d, down_d, xs):
    hT, ident, par = mem["hT"], mem["ident"], mem["par"]
    wts, base, arena = (mem[n] for n in ("wts", "base", "arena"))
    iota = mem["iota"]
    w, ow, cos, sin, wr, sgu, sd = (mem[n] for n in ("w", "ow", "cos", "sin", "wr", "shared_gu", "shared_d"))

    def pc(name, k=0):
        return par[:, PAR[name] + k:PAR[name] + k + 1]

    with ExitStack() as ctx:
        def sb(name, shape, dt=F32):
            return ctx.enter_context(nc.sbuf_tensor(name, shape, dt))

        at_column = [0]

        def carve(*shape):
            n = math.prod(shape)
            v = arena[:, at_column[0]:at_column[0] + n]
            at_column[0] += n
            names = [f"d{k}" for k in range(len(shape))]
            return v.rearrange(f"p ({' '.join(names)}) -> p {' '.join(names)}", **dict(zip(names[1:], shape[1:])))

        pb = sb("proj_bias", [P, 6])
        cw1 = sb("conv_mid", [P, 6])
        mhalf, eps = sb("minus_half", [P, TJ]), sb("eps", [P, TJ])
        hcur = sb("h_cur", [P, T])
        spare = sb("spare", [1, 1])
        xn = sb("h_norm_tok", [P, TJ, P])
        y = sb("h_norm2_tok", [P, TJ, P])
        st = [sb(f"ln_stats{n}", [P, TJ, 6]) for n in range(4)]
        mv = [sb(f"ln_mv{n}", [P, TJ, 2]) for n in range(4)]
        ve = [sb(f"ln_var{n}", [P, TJ]) for n in range(4)]
        rs = [sb(f"ln_rstd{n}", [P, TJ]) for n in range(4)]
        yT = sb("y_T", [P, 2, T])
        hb = carve(2, 5, T + 2)
        cv = carve(2, 5, T)
        zs = carve(2, T)
        ra, rb = carve(2, T), carve(2, T)
        rc, rd = ra, rb
        q4 = carve(2, 4, T)
        tok = carve(2, 5, TJ, P)
        at = sb("attn_T", [P, TJ, P])
        lkv = sb("lin_kv", [P, 4, P])
        um, pr = sb("gate_arg", [P, 2, T]), sb("gate_prod", [P, 2, T])
        th, gt = um, pr
        gn = sb("gated_norm_tok", [P, TJ, H])
        gT = sb("gated_norm_T", [P, 2, T])
        ho = sb("out_silu", [P, T + 2])
        oc = sb("out_conv", [P, T])
        h4 = sb("r_h_cur", [P, T])
        xf = sb("xf_tok", [P, 2, TJ, D])
        rows = sb("scatter_rows", [P, 2, TJ, ROW])
        places = sb("places", [P, TILES, K])
        tmp = sb("r_tmp", [P, TJ * K, NE])
        xfT = sb("xf_T", [P, 2, T])
        nmax, esum, erec = sb("r_nmax", [P, TJ]), sb("r_esum", [P, TJ]), sb("r_erec", [P, TJ])
        ex, probs = sb("r_exp", [P, TJ, NE]), sb("r_probs", [P, TJ, NE])
        top, topi = sb("r_top", [P, TJ, 8]), sb("r_topi", [P, TJ, 8], U32)
        tsum, trec = sb("r_tsum", [P, TJ]), sb("r_trec", [P, TJ])
        idxf = sb("r_idxf", [P, TJ, K])
        one = sb("r_onehot", [P, TJ * K, NE], BF16)
        took = sb("r_took", [P, TJ, NE], BF16)
        pos = sb("r_pos", [P, TJ, NE])
        slf = sb("r_slot", [P, TJ * K])
        sli = sb("r_slot_int", [P, 2, TJ * K], I32)
        pspare = sb("r_pool_spare", [1, 1])
        before, ones = sb("r_before", [P, P], BF16), sb("r_ones", [P, P], BF16)
        sg, hs = sb("r_silu", [P, NS, T]), sb("r_hidden", [P, NS, T])

        def ps(name):
            return ctx.enter_context(nc.psum_tensor(name, [P, 512], F32))

        with ExitStack() as setup:
            psB = setup.enter_context(nc.psum_tensor("ps_bias", [P, 512], F32))
            block = setup.enter_context(nc.Block())
            folded, bias_mm, biased = sem("w_folded"), sem("bias_mm"), sem("bias_added")
            cleared, halved = sem("rows_cleared"), sem("gamma_scaled")

            @block.gpsimd
            def _(pool):
                nc.gpsimd.memset(hb[:, :, :, 0:1], 0.0).then_inc(cleared, 1)
                nc.gpsimd.memset(hb[:, :, :, T + 1:T + 2], 0.0).then_inc(cleared, 1)
                nc.gpsimd.memset(ho[:, 0:1], 0.0).then_inc(cleared, 1)
                nc.gpsimd.memset(ho[:, T + 1:T + 2], 0.0).then_inc(cleared, 1)
                nc.gpsimd.memset(at[:, :, :], 0.0).then_inc(cleared, 1)
                nc.gpsimd.memset(mhalf[:, :], -0.5).then_inc(cleared, 1)
                nc.gpsimd.memset(eps[:, :], EPS).then_inc(cleared, 1)
                nc.gpsimd.memset(ones[:, :], 1.0).then_inc(cleared, 1)
                nc.gpsimd.memset(before[:, :], 1.0).then_inc(cleared, 1)
                nc.gpsimd.iota(iota[:, :], [[1, NE]], base=0, channel_multiplier=0,
                               allow_small_or_imprecise_dtypes=True).then_inc(cleared, 1)
                nc.gpsimd.iota(base[:, :], [[REGION, NE]], base=0, channel_multiplier=0,
                               allow_small_or_imprecise_dtypes=True).then_inc(cleared, 1)
                nc.gpsimd.iota(places[:, :, :], [[P * K, TILES], [1, K]], base=PLACE0, channel_multiplier=K,
                               allow_small_or_imprecise_dtypes=True).then_inc(cleared, 1)
                pool.wait_ge(cleared, 12)
                nc.gpsimd.affine_select(out=before[:, :], in_=before[:, :], compare_op=ALU.is_gt, fill=0.0, base=0,
                                        pattern=[[1, P]], channel_multiplier=-1).then_inc(cleared, 1)
                pool.wait_ge(cleared, 13)

            @block.tensor
            def _(pe):
                pe.wait_ge(w_loaded, 112)
                for c in range(5):
                    nc.tensor.matmul(psB[:, c:c + 1], w[:, c * P:(c + 1) * P], pc("ln_b", c // 2),
                                     start=True, stop=True)
                for f in range(2):
                    mm = nc.tensor.matmul(psB[:, 5:6], ow[:, f, :], pc("out_lb", f), start=(f == 0), stop=(f == 1))
                mm.then_inc(bias_mm, 1)

            @block.vector
            def _(dve):
                dve.wait_ge(w_loaded, 112)
                dve.wait_ge(bias_mm, 1)
                for c in range(5):
                    nc.vector.tensor_scalar(w[:, c * P:(c + 1) * P], w[:, c * P:(c + 1) * P], pc("ln_g", c // 2),
                                            None, ALU.mult).then_inc(folded, 1)
                for f in range(2):
                    nc.vector.tensor_scalar(ow[:, f, :], ow[:, f, :], pc("out_g", f), None, ALU.mult)\
                      .then_inc(folded, 1)
                nc.vector.tensor_scalar(cw1[:, 0:5], par[:, PAR["cw1"]:PAR["cw1"] + 5], 1.0, None, ALU.add)\
                  .then_inc(folded, 1)
                nc.vector.tensor_scalar(cw1[:, 5:6], pc("out_cw", 1), 1.0, None, ALU.add).then_inc(folded, 1)
                for name in ("gamma", "beta", "gamma_sw", "beta_sw"):
                    nc.vector.tensor_scalar(pc(name, QQ), pc(name, QQ), 1.0 / G, None, ALU.mult).then_inc(halved, 1)
                nc.vector.tensor_tensor(pb[:, 0:5], psB[:, 0:5], par[:, PAR["proj_b"]:PAR["proj_b"] + 5], ALU.add)\
                  .then_inc(biased, 1)
                nc.vector.tensor_tensor(pb[:, 5:6], psB[:, 5:6], pc("out_b"), ALU.add).then_inc(biased, 1)
                dve.wait_ge(folded, 9)
                dve.wait_ge(halved, 4)
                dve.wait_ge(biased, 2)

        psT, psR = ps("ps_ln_in"), ps("ps_ln_out")
        ring = [ps(f"ps_ring{n}") for n in range(2)]
        psQ = [ps(f"ps_out{n}") for n in range(4)]
        plan_pool, plan_dve, plan_pe, plan_sp, plan_act = plan(nc, mem, sem, ctx, xs, psR)
        block = ctx.enter_context(nc.Block())

        gu_loaded = sem("gu_loaded")
        h4_taken, h4_tok, r_back, r_copied, logits = (
            sem("r_" + n) for n in ("h_taken", "h_tok", "back", "copied", "logits"))
        maxed, exped, inv, prob, topped = (sem("r_maxed"), sem("r_exped"), sem("r_inv"), sem("r_prob_ok"),
                                           sem("r_topped"))
        indexed, floated, tsummed, tinv, weighed = (sem("r_indexed"), sem("r_floated"), sem("r_tsummed"),
                                                    sem("r_tinv"), sem("r_weighed"))
        onehot, taken, ranked, placed, moved = (sem("r_onehot_ok"), sem("r_taken"), sem("r_ranked"),
                                                sem("r_placed"), sem("base_moved"))
        masked, summed, slotted = sem("r_masked"), sem("r_summed"), sem("r_slotted")
        noted = sem("r_noted")
        carried, rows_copied = sem("r_carried"), sem("r_rows_copied")
        scattered = [sem(f"r_scattered{q}") for q in range(2)]
        gate_mm, up_mm, r_gated, hidden, shared_mm, shared_add = (
            sem("r_" + n) for n in ("gate_mm", "up_mm", "gated_ok", "hidden_ok", "shared_mm", "shared_add"))

        def sent(q, b):
            return b // 2 * (16 * TJ * K) if isinstance(b, int) else (b - q) * (8 * TJ * K)

        h_taken = sem("h_taken")
        h_tok = sem("h_tok")
        stats = [sem(f"ln{n}_stats") for n in range(4)]
        aggr = [sem(f"ln{n}_aggr") for n in range(4)]
        var_eps = [sem(f"ln{n}_var_eps") for n in range(4)]
        rstd = [sem(f"ln{n}_rstd") for n in range(4)]
        norm = [sem(f"ln{n}_norm") for n in range(4)]
        xn_back, based = sem("xn_back"), sem("h_based")
        y_back, y_copied = sem("y_back"), sem("y_copied")
        ring_full, ring_used = sem("ring_full"), sem("ring_used")
        mid, left, conv = sem("conv_mid_done"), sem("conv_left"), sem("conv_done")
        swapped, rot_in, rot_c, rot_d, rotated = (sem("z_swapped_ok"), sem("rot_in"), sem("rot_cos"),
                                                 sem("rot_sin"), sem("rotated"))
        attned_half = sem("attn_relu")
        sims, attned, kv_mm, kv_copied = sem("sims"), sem("attned"), sem("kv_mm"), sem("kv_copied")
        hats, gate_arg, gate_tanh, gate_prod, gated = (sem("hats"), sem("gate_arg_ok"), sem("gate_tanh_ok"),
                                                      sem("gate_prod_ok"), sem("gated_ok"))
        g_tok, g_back, g_copied = sem("g_tok"), sem("g_back"), sem("g_copied")
        o_mm, o_silu, o_mid, o_left, o_conv, added = (sem("o_mm"), sem("o_silu"), sem("o_mid"), sem("o_left"),
                                                     sem("o_conv"), sem("h_added"))
        CORD = [4, 0, 1, 2, 3]

        @block.sync
        def _(sp):
            sp.wait_ge(added, B)
            sp.wait_ge(g_back, 2 * B)
            for e in range(0, NE, 16):
                sp.dma_start(mem["gu"][:, e * 2 * F:(e + 16) * 2 * F],
                             gu_d[:, e:e + 16].rearrange("p e a f -> p (e a f)")).then_inc(gu_loaded, 16)
                sp.dma_start(mem["down"][:, e * D:(e + 16) * D],
                             down_d[:, e:e + 16].rearrange("p e d -> p (e d)")).then_inc(gu_loaded, 16)
            plan_sp(sp)
            sp.wait_ge(gu_loaded, 16 * 2 * (NE // 16))

        @block.tensor
        def _(pe):
            def s1a(b, q):
                pe.wait_ge(h_taken, b + 1)
                need(pe, moved, b - 3 + before_in_turn((4, "d"), (1, "a")))
                for j in range(TJ):
                    mm = nc.tensor.transpose(psT[:, j * P:(j + 1) * P], hcur[:, j * P:(j + 1) * P], ident[:, :])
                mm.then_inc(h_tok, 1)

            def s1b(b, q):
                pe.wait_ge(norm[0], b + 1)
                need(pe, y_copied, b)
                for j in range(TJ):
                    mm = nc.tensor.transpose(psR[:, j * P:(j + 1) * P], xn[:, j, :], ident[:, :])
                mm.then_inc(xn_back, 1)

            def s1c(b, q):
                pe.wait_ge(norm[1], b + 1)
                pe.wait_ge(based, b + 1)
                for j in range(TJ):
                    mm = nc.tensor.transpose(psR[:, j * P:(j + 1) * P], y[:, j, :], ident[:, :])
                mm.then_inc(y_back, 1)

            def s2a(b, q, k):
                c = CORD[k]
                if k == 0:
                    pe.wait_ge(y_copied, b + 1)
                need(pe, ring_used, b * 10 + (k - 1))
                nc.tensor.matmul(ring[k % 2][:, :], w[:, c * P:(c + 1) * P], yT[:, q, :], start=True, stop=True)\
                  .then_inc(ring_full, 1)

            def s2b(b, q, k):
                for c in (k,):
                    if c == LK:
                        pe.wait_ge(rotated, b * 4 + 4)
                    else:
                        pe.wait_ge(conv, b * 5 + CORD.index(c) + 1)
                    pe.wait_ge(ring_used, b * 10 + 4 + k)
                    src = q4[:, q, KL, :] if c == LK else cv[:, q, c, :]
                    for j in range(TJ):
                        mm = nc.tensor.transpose(ring[(5 + k) % 2][:, j * P:(j + 1) * P], src[:, j * P:(j + 1) * P],
                                                 ident[:, :])
                    mm.then_inc(ring_full, 1)

            def s3a(b, q):
                pe.wait_ge(rotated, b * 4 + 4)
                need(pe, hidden, (b - 1 + before_in_turn((4, "s"), (3, "a"))) * NS)
                for j in range(TJ):
                    mm = nc.tensor.matmul(psQ[0][:, j * P:(j + 1) * P], q4[:, q, QK, j * P:(j + 1) * P],
                                          q4[:, q, QQ, j * P:(j + 1) * P], start=True, stop=True)
                mm.then_inc(sims, 1)
                pe.wait_ge(ring_used, b * 10 + 10)
                need(pe, shared_add, b - 1 + before_in_turn((4, "t"), (3, "a")))
                for j in range(TJ):
                    mm = nc.tensor.matmul(psQ[1][:, :], tok[:, q, LK, j, :], tok[:, q, 0:4, j, :],
                                          start=(j == 0), stop=(j == TJ - 1))
                mm.then_inc(kv_mm, 1)

            def s3b(b, q, m):
                if m == 0:
                    pe.wait_ge(attned, b + 1)
                    pe.wait_ge(kv_copied, b + 1)
                for c in ((V0, V0 + 1), (U0, U0 + 1))[m]:
                    for j in range(TJ):
                        nc.tensor.matmul(psQ[c][:, j * P:(j + 1) * P], tok[:, q, c, j, :], at[:, j, :],
                                         start=(j == 0), stop=False, skip_group_check=True)
                    mm = nc.tensor.matmul(psQ[c][:, :], lkv[:, c, :], q4[:, q, LQ, :], start=False, stop=True,
                                          skip_group_check=True)
                    mm.then_inc(hats, 1)

            def s3c(b, q):
                pe.wait_ge(gated, b * 2 + 2)
                for j in range(TJ):
                    for f in range(2):
                        mm = nc.tensor.transpose(psQ[j // 2][:, (j % 2) * H + f * P:(j % 2) * H + (f + 1) * P],
                                                 gt[:, f, j * P:(j + 1) * P], ident[:, :])
                mm.then_inc(g_tok, 1)

            def s3n(b, q):
                pe.wait_ge(norm[2], b + 1)
                for f in range(2):
                    for j in range(TJ):
                        mm = nc.tensor.transpose(psQ[2 + f][:, j * P:(j + 1) * P], gn[:, j, f * P:(f + 1) * P],
                                                 ident[:, :])
                    mm.then_inc(g_back, 1)

            def s3d(b, q):
                pe.wait_ge(g_copied, b * 2 + 2)
                for f in range(2):
                    mm = nc.tensor.matmul(psQ[0][:, :], ow[:, f, :], gT[:, f, :], start=(f == 0), stop=(f == 1))
                mm.then_inc(o_mm, 1)

            def s4a(b, q):
                pe.wait_ge(h4_taken, b + 1)
                pe.wait_ge(norm[0], upto(b, 2 + before_in_turn((1, "n"), (4, "a"))))
                for j in range(TJ):
                    mm = nc.tensor.transpose(psT[:, j * P:(j + 1) * P], h4[:, j * P:(j + 1) * P], ident[:, :])
                mm.then_inc(h4_tok, 1)

            def s4b(b, q):
                pe.wait_ge(norm[3], b + 1)
                for j in range(TJ):
                    mm = nc.tensor.transpose(psT[:, j * P:(j + 1) * P], xf[:, q, j, :], ident[:, :])
                mm.then_inc(r_back, 1)

            def s4c(b, q):
                pe.wait_ge(r_copied, b + 1)
                for j in range(TJ):
                    mm = nc.tensor.matmul(psT[:, j * NE:(j + 1) * NE], xfT[:, q, j * P:(j + 1) * P], wr[:, :],
                                          start=True, stop=True)
                mm.then_inc(logits, 1)

            def s4d(b, q):
                pe.wait_ge(taken, b + 1)
                for j in range(TJ):
                    for i in range(j):
                        nc.tensor.matmul(psT[:, j * NE:(j + 1) * NE], ones[:, :], took[:, i, :],
                                         start=(i == 0), stop=False)
                    nc.tensor.matmul(psT[:, j * NE:(j + 1) * NE], before[:, :], took[:, j, :],
                                     start=(j == 0), stop=True)
                for j in range(TJ):
                    mm = nc.tensor.matmul(psT[:, TJ * NE:(TJ + 1) * NE], ones[:, :], took[:, j, :],
                                          start=(j == 0), stop=(j == TJ - 1))
                mm.then_inc(ranked, 1)

            def s4s(b, q):
                pe.wait_ge(r_copied, b + 1)
                pe.wait_ge(o_silu, upto(b, before_in_turn((3, "d"), (4, "s"))))
                for s in range(NS):
                    nc.tensor.matmul(psQ[1 + 2 * s][:, :], sgu[:, s, 0, :], xfT[:, q, :], start=True, stop=True)\
                      .then_inc(gate_mm, 1)
                    nc.tensor.matmul(psQ[2 - 2 * s][:, :], sgu[:, s, 1, :], xfT[:, q, :], start=True, stop=True)\
                      .then_inc(up_mm, 1)

            def s4t(b, q):
                pe.wait_ge(hidden, b * NS + NS)
                for j in range(TJ):
                    out = psQ[1][:, j * P:(j + 1) * P]
                    nc.tensor.matmul(out, h4[:, j * P:(j + 1) * P], ident[:, :], start=True, stop=False)
                    nc.tensor.matmul(out, ident[:, :], xf[:, q, j, :], start=False, stop=False)
                    for s in range(NS):
                        mm = nc.tensor.matmul(out, hs[:, s, j * P:(j + 1) * P], sd[:, s, :],
                                              start=False, stop=(s == NS - 1))
                mm.then_inc(shared_mm, 1)

            batch_pipeline(pe, {1: {"a": s1a, "b": s1b, "c": s1c}, 2: {"a": s2a, "b": s2b},
                                3: {"a": s3a, "b": s3b, "c": s3c, "n": s3n, "d": s3d},
                                4: {"a": s4a, "b": s4b, "c": s4c, "d": s4d, "s": s4s, "t": s4t}}, ORDER)
            plan_pe(pe)

        @block.scalar
        def _(act):
            def s1c(b, q):
                act.wait_ge(y_back, b + 1)
                need(act, ring_full, (b - 1) * 10 - 5)
                nc.scalar.activation(yT[:, q, :], psR[:, :], ACT.Copy).then_inc(y_copied, 1)

            def s2a(b, q, k):
                def middle(k, c):
                    act.wait_ge(ring_used, b * 10 + k + 1)
                    nc.scalar.activation(cv[:, q, c, :], hb[:, q, c, 1:T + 1], ACT.Identity, scale=cw1[:, c:c + 1],
                                         bias=pc("cb", c)).then_inc(mid, 1)

                if k == 0:
                    need(act, hats, (b - 1) * 4)
                    need(act, gated, (b - 1) * 2)
                    need(act, ring_used, (b - 1) * 10)
                    need(act, ring_full, (b - 1) * 10)
                    need(act, conv, (b - 1) * 5)
                    need(act, rotated, (b - 1) * 4)
                c = CORD[k]
                act.wait_ge(ring_full, b * 10 + k + 1)
                nc.scalar.activation(hb[:, q, c, 1:T + 1], ring[k % 2][:, :], ACT.Silu, bias=pb[:, c:c + 1])\
                  .then_inc(ring_used, 1)
                if k:
                    middle(k - 1, CORD[k - 1])
                if k == 4:
                    middle(4, CORD[4])

            def s2b(b, q, k):
                def rot(i):
                    if i == 0:
                        act.wait_ge(conv, b * 5 + 1)
                        act.wait_ge(swapped, b + 1)
                    need(act, rotated, b * 4 + i - 1)
                    nc.scalar.activation(ra[:, i % 2, :], cv[:, q, 4, :], ACT.Identity, scale=pc("gamma", i),
                                         bias=pc("beta", i)).then_inc(rot_in, 1)
                    nc.scalar.activation(rb[:, i % 2, :], zs[:, q, :], ACT.Identity, scale=pc("gamma_sw", i),
                                         bias=pc("beta_sw", i)).then_inc(rot_in, 1)

                def to_tok(k, c):
                    act.wait_ge(ring_full, b * 10 + 5 + k + 1)
                    nc.scalar.activation(tok[:, q, c, :, :].rearrange("p j e -> p (j e)"), ring[(5 + k) % 2][:, :],
                                         ACT.Copy).then_inc(ring_used, 1)

                if k < 4:
                    rot(k)
                to_tok(k, k)

            def s3a(b, q):
                act.wait_ge(kv_mm, b + 1)
                need(act, hats, b * 4)
                nc.scalar.activation(lkv[:, :, :].rearrange("p c e -> p (c e)"), psQ[1][:, :], ACT.Copy,
                                     scale=1.0 / T).then_inc(kv_copied, 1)

            def s3b(b, q, m):
                for f in range(2) if m == 0 else ():
                    act.wait_ge(gate_arg, b * 2 + f + 1)
                    need(act, gated, b * 2)
                    nc.scalar.activation(th[:, f, :], um[:, f, :], ACT.Tanh, scale=0.5).then_inc(gate_tanh, 1)

            def s3n(b, q):
                for f in range(2):
                    act.wait_ge(g_back, b * 2 + f + 1)
                    need(act, o_mm, b)
                    nc.scalar.activation(gT[:, f, :], psQ[2 + f][:, :], ACT.Copy).then_inc(g_copied, 1)

            def s3d(b, q):
                act.wait_ge(o_mm, b + 1)
                need(act, o_conv, b)
                nc.scalar.activation(ho[:, 1:T + 1], psQ[0][:, :], ACT.Silu, bias=pb[:, 5:6]).then_inc(o_silu, 1)
                act.wait_ge(o_silu, b + 1)
                need(act, added, b)
                nc.scalar.activation(oc[:, :], ho[:, 1:T + 1], ACT.Identity, scale=cw1[:, 5:6],
                                     bias=pc("out_cb")).then_inc(o_mid, 1)

            def s4a(b, q):
                act.wait_ge(added, b + 1)
                need(act, shared_mm, b)
                nc.scalar.activation(h4[:, :], hT[:, bass.ds(b * T, T)], ACT.Copy).then_inc(h4_taken, 1)

            def s4b(b, q):
                act.wait_ge(r_back, b + 1)
                need(act, up_mm, (b - 1) * NS)
                nc.scalar.activation(xfT[:, q, :], psT[:, :], ACT.Copy).then_inc(r_copied, 1)
                need(act, scattered[q], sent(q, b))
                nc.scalar.activation(rows[:, q, :, 0:D], xf[:, q], ACT.Copy).then_inc(rows_copied, 1)

            def s4c(b, q):
                act.wait_ge(maxed, b + 1)
                need(act, prob, b)
                for j in range(TJ):
                    nc.scalar.activation(ex[:, j, :], psT[:, j * NE:(j + 1) * NE], ACT.Exp, bias=nmax[:, j:j + 1],
                                         accum_out=esum[:, j:j + 1]).then_inc(exped, 1)

            def s4s(b, q):
                for s in range(NS):
                    act.wait_ge(gate_mm, b * NS + s + 1)
                    need(act, hidden, b * NS)
                    nc.scalar.activation(sg[:, s, :], psQ[1 + 2 * s][:, :], ACT.Silu).then_inc(r_gated, 1)

            def s4t(b, q):
                act.wait_ge(shared_mm, b + 1)
                nc.scalar.activation(hT[:, bass.ds(b * (TJ * D), TJ * D)], psQ[1][:, :], ACT.Copy)\
                  .then_inc(shared_add, 1)

            batch_pipeline(act, {1: {"c": s1c}, 2: {"a": s2a, "b": s2b},
                                 3: {"a": s3a, "b": s3b, "n": s3n, "d": s3d},
                                 4: {"a": s4a, "b": s4b, "c": s4c, "s": s4s, "t": s4t}}, ORDER)
            plan_act(act)

        @block.gpsimd
        def _(pool):
            def inverse_root(n, b):
                pool.wait_ge(aggr[n], b + 1)
                nc.gpsimd.tensor_tensor(ve[n][:, :], mv[n][:, :, 1], eps[:, :], ALU.add).then_inc(var_eps[n], 1)
                pool.wait_ge(var_eps[n], b + 1)
                need(pool, norm[n], b)
                nc.gpsimd.tensor_tensor(rs[n][:, :], ve[n][:, :], mhalf[:, :], ALU.pow).then_inc(rstd[n], 1)

            def s1a(b, q):
                need(pool, h_tok, b)
                need(pool, based, b)
                nc.gpsimd.tensor_copy(hcur[:, :], hT[:, bass.ds(b * T, T)]).then_inc(h_taken, 1)
                inverse_root(0, b)

            def s1b(b, q):
                inverse_root(1, b)

            def s2b(b, q, k):
                for i in (k,) if k < 4 else ():
                    pool.wait_ge(rot_in, b * 8 + 2 * i + 2)
                    need(pool, rotated, b * 4 + i - 1)
                    nc.gpsimd.tensor_tensor(rc[:, i % 2, :], ra[:, i % 2, :], cos[:, :], ALU.mult).then_inc(rot_c, 1)

            def s3c(b, q):
                inverse_root(2, b)

            def s3d(b, q):
                pool.wait_ge(o_conv, b + 1)
                pool.wait_ge(based, b + 1)
                nc.gpsimd.tensor_tensor(hT[:, bass.ds(b * T, T)], hT[:, bass.ds(b * T, T)], oc[:, :], ALU.add)\
                  .then_inc(added, 1)
                if isinstance(b, int) and b == B - 1:
                    pool.wait_ge(added, B)

            def s4a(b, q):
                inverse_root(3, b)

            def s4d(b, q):
                pool.wait_ge(placed, b + 1)
                need(pool, summed, b)
                nc.gpsimd.tensor_tensor(tmp[:, :, :].rearrange("p (j k) e -> p j k e", j=TJ),
                                        one[:, :, :].rearrange("p (j k) e -> p j k e", j=TJ),
                                        pos[:, :, :].unsqueeze(2).to_broadcast([P, TJ, K, NE]), ALU.mult)\
                  .then_inc(masked, 1)

            def s5e(b, q, k):
                if k == 0:
                    need(pool, carried, b)
                    pool.wait_ge(rows_copied, b + 1)
                    pool.wait_ge(slotted, b + 1)
                    pool.wait_ge(noted, b * 2 + 2)
                    nc.gpsimd.tensor_tensor(pspare[:, :], eps[0:1, 0:1], eps[0:1, 0:1], ALU.add).then_inc(carried, 1)
                for c in range(k * (TJ * K // SENDS), (k + 1) * (TJ * K // SENDS)):
                    nc.gpsimd.indirect_dma_start(
                        out=xs, out_offset=bass.IndirectOffsetOnAxis(ap=sli[:, q, c:c + 1], axis=0),
                        in_=rows[:, q, c // K, :], in_offset=None).then_inc(scattered[q], 16)

            plan_pool(pool)
            batch_pipeline(pool, {1: {"a": s1a, "b": s1b}, 2: {"b": s2b}, 3: {"c": s3c, "d": s3d},
                                  4: {"a": s4a, "d": s4d}, 5: {"e": s5e}}, ORDER)
            for q in range(2):
                pool.wait_ge(scattered[q], 16 * TJ * K * (B // 2))

        @block.vector
        def _(dve):
            def statistics(n, b, src, width):
                for j in range(TJ):
                    nc.vector.bn_stats(st[n][:, j, :], src(j)).then_inc(stats[n], 1)
                dve.wait_ge(stats[n], b * TJ + TJ)
                nc.vector.memset(spare[:, :], 0.0)
                for j in range(TJ):
                    ins = nc.vector.bn_aggr(mv[n][:, j, :], st[n][:, j, :])
                    if j == TJ - 1:
                        ins.then_inc(aggr[n], 1)

            def normalise(n, b, dst, src):
                dve.wait_ge(rstd[n], b + 1)
                for j in range(TJ):
                    ins = nc.vector.tensor_scalar(dst[:, j, :], src(j), mv[n][:, j, 0:1], rs[n][:, j:j + 1],
                                                  ALU.subtract, ALU.mult)
                ins.then_inc(norm[n], 1)

            def s1a(b, q):
                dve.wait_ge(h_tok, b + 1)
                statistics(0, b, lambda j: psT[:, j * P:(j + 1) * P], P)

            def s1n(b, q):
                need(dve, xn_back, b)
                normalise(0, b, xn, lambda j: psT[:, j * P:(j + 1) * P])

            def s1b(b, q):
                dve.wait_ge(norm[0], b + 1)
                statistics(1, b, lambda j: xn[:, j, :], P)

            def s1m(b, q):
                need(dve, y_back, b)
                normalise(1, b, y, lambda j: xn[:, j, :])
                dve.wait_ge(xn_back, b + 1)
                nc.vector.tensor_tensor(hT[:, bass.ds(b * T, T)], hcur[:, :], psR[:, :], ALU.add).then_inc(based, 1)

            def s2a(b, q, k):
                for c in (CORD[k],):
                    dve.wait_ge(mid, b * 5 + k + 1)
                    nc.vector.scalar_tensor_tensor(out=cv[:, q, c, :], in0=hb[:, q, c, 0:T], scalar=pc("cw0", c),
                                                   in1=cv[:, q, c, :], op0=ALU.mult, op1=ALU.add).then_inc(left, 1)
                    dve.wait_ge(left, b * 5 + k + 1)
                    nc.vector.scalar_tensor_tensor(out=cv[:, q, c, :], in0=hb[:, q, c, 2:T + 2], scalar=pc("cw2", c),
                                                   in1=cv[:, q, c, :], op0=ALU.mult, op1=ALU.add).then_inc(conv, 1)
                    if k == 0:
                        dve.wait_ge(conv, b * 5 + 1)
                        need(dve, rot_in, (b - 1) * 8)
                        nc.vector.memset(spare[:, :], 0.0)
                        nc.vector.stream_shuffle(zs[:, q, :], cv[:, q, 4, :], [i ^ 1 for i in range(32)])\
                          .then_inc(swapped, 1)

            def s2b(b, q, k):
                if k == 0:
                    need(dve, hats, (b - 1) * 4)
                    need(dve, ring_full, (b - 1) * 10)
                for i in (k,) if k < 4 else ():
                    dve.wait_ge(rot_in, b * 8 + 2 * i + 2)
                    nc.vector.tensor_tensor(rd[:, i % 2, :], rb[:, i % 2, :], sin[:, :], ALU.mult).then_inc(rot_d, 1)
                    dve.wait_ge(rot_d, b * 4 + i + 1)
                    dve.wait_ge(rot_c, b * 4 + i + 1)
                    nc.vector.tensor_tensor(q4[:, q, i, :], rc[:, i % 2, :], rd[:, i % 2, :], ALU.add)\
                      .then_inc(rotated, 1)

            def s3a(b, q):
                dve.wait_ge(sims, b + 1)
                need(dve, hats, b * 4)
                for g in range(P // G):
                    r = slice(g * G, (g + 1) * G)
                    s = psQ[0][r, :].rearrange("p (j i) -> p j i", j=TJ)[:, :, r]
                    ins = nc.vector.tensor_scalar(at[r, :, r], s, 0.0, None, ALU.max)
                    ins.then_inc(attned_half, 1)
                dve.wait_ge(attned_half, b * 2 + 2)
                for g in range(P // G):
                    r = slice(g * G, (g + 1) * G)
                    ins = nc.vector.tensor_tensor(at[r, :, r], at[r, :, r], at[r, :, r], ALU.mult)
                ins.then_inc(attned, 1)

            def s3b(b, q, m):
                for f in range(2) if m == 0 else ():
                    dve.wait_ge(hats, b * 4 + f + 1)
                    need(dve, gate_tanh, b * 2)
                    nc.vector.tensor_tensor(um[:, f, :], psQ[V0 + f][:, :], cv[:, q, U0 + f, :], ALU.mult)\
                      .then_inc(gate_arg, 1)
                for f in range(2) if m == 1 else ():
                    dve.wait_ge(hats, b * 4 + 2 + f + 1)
                    nc.vector.scalar_tensor_tensor(out=pr[:, f, :], in0=psQ[U0 + f][:, :], scalar=0.5,
                                                   in1=cv[:, q, V0 + f, :], op0=ALU.mult, op1=ALU.mult)\
                      .then_inc(gate_prod, 1)
                    dve.wait_ge(gate_prod, b * 2 + f + 1)
                    dve.wait_ge(gate_tanh, b * 2 + f + 1)
                    need(dve, g_tok, b)
                    nc.vector.scalar_tensor_tensor(out=gt[:, f, :], in0=th[:, f, :], scalar=1.0, in1=pr[:, f, :],
                                                   op0=ALU.add, op1=ALU.mult).then_inc(gated, 1)

            def gated_tok(j):
                return psQ[j // 2][:, (j % 2) * H:(j % 2 + 1) * H]

            def s3c(b, q):
                dve.wait_ge(g_tok, b + 1)
                statistics(2, b, gated_tok, H)

            def s3n(b, q):
                need(dve, g_back, b * 2)
                normalise(2, b, gn, gated_tok)

            def s3d(b, q):
                dve.wait_ge(o_mid, b + 1)
                nc.vector.scalar_tensor_tensor(out=oc[:, :], in0=ho[:, 0:T], scalar=pc("out_cw", 0), in1=oc[:, :],
                                               op0=ALU.mult, op1=ALU.add).then_inc(o_left, 1)
                dve.wait_ge(o_left, b + 1)
                nc.vector.scalar_tensor_tensor(out=oc[:, :], in0=ho[:, 2:T + 2], scalar=pc("out_cw", 2), in1=oc[:, :],
                                               op0=ALU.mult, op1=ALU.add).then_inc(o_conv, 1)

            def s4a(b, q):
                dve.wait_ge(h4_tok, b + 1)
                statistics(3, b, lambda j: psT[:, j * P:(j + 1) * P], P)

            def s4n(b, q):
                need(dve, rows_copied, b - 1)
                need(dve, r_back, b - 1)
                need(dve, shared_mm, b - 1)
                normalise(3, b, xf[:, q], lambda j: psT[:, j * P:(j + 1) * P])

            def s4c(b, q):
                dve.wait_ge(logits, b + 1)
                g3 = psT[:, 0:TJ * NE].rearrange("p (j e) -> p j e", j=TJ)
                nc.vector.tensor_reduce(nmax[:, :], g3, AX.X, ALU.max, negate=True).then_inc(maxed, 1)

            def s4g(b, q):
                dve.wait_ge(exped, b * TJ + TJ)
                nc.vector.reciprocal(erec[:, :], esum[:, :]).then_inc(inv, 1)
                dve.wait_ge(inv, b + 1)
                nc.vector.tensor_tensor(probs[:, :, :], ex[:, :, :],
                                        erec[:, :].unsqueeze(2).to_broadcast([P, TJ, NE]), ALU.mult).then_inc(prob, 1)
                dve.wait_ge(prob, b + 1)
                nc.vector.memset(spare[:, :], 0.0)
                for j in range(TJ):
                    nc.vector.max(top[:, j, :], probs[:, j, :]).then_inc(topped, 1)
                dve.wait_ge(topped, b * TJ + TJ)
                nc.vector.memset(spare[:, :], 0.0)
                for j in range(TJ):
                    nc.vector.max_index(topi[:, j, :], top[:, j, :], probs[:, j, :]).then_inc(indexed, 1)
                nc.vector.tensor_reduce(tsum[:, :], top[:, :, 0:K], AX.X, ALU.add).then_inc(tsummed, 1)
                dve.wait_ge(indexed, b * TJ + TJ)
                nc.vector.tensor_copy(idxf[:, :, :], topi[:, :, 0:K]).then_inc(floated, 1)
                dve.wait_ge(tsummed, b + 1)
                nc.vector.reciprocal(trec[:, :], tsum[:, :]).then_inc(tinv, 1)
                dve.wait_ge(floated, b + 1)
                need(dve, masked, b)
                nc.vector.tensor_tensor(one[:, :, :],
                                        idxf[:, :, :].rearrange("p j k -> p (j k)").unsqueeze(2)
                                        .to_broadcast([P, TJ * K, NE]),
                                        iota[:, :].unsqueeze(1).to_broadcast([P, TJ * K, NE]),
                                        ALU.is_equal).then_inc(onehot, 1)
                dve.wait_ge(tinv, b + 1)
                nc.vector.tensor_tensor(wts[:, bass.ds(b * (TJ * K), TJ * K)].rearrange("p (j k) -> p j k", j=TJ),
                                        top[:, :, 0:K], trec[:, :].unsqueeze(2).to_broadcast([P, TJ, K]), ALU.mult)\
                  .then_inc(weighed, 1)
                dve.wait_ge(onehot, b + 1)
                need(dve, ranked, b)
                with nc.allow_low_precision("sums of at most six ones"):
                    nc.vector.tensor_reduce(took[:, :, :], one[:, :, :].rearrange("p (j k) e -> p j e k", j=TJ),
                                            AX.X, ALU.add).then_inc(taken, 1)

            def s4d(b, q):
                dve.wait_ge(ranked, b + 1)
                need(dve, moved, b)
                need(dve, masked, b)
                nc.vector.tensor_tensor(pos[:, :, :], psT[:, 0:TJ * NE].rearrange("p (j e) -> p j e", j=TJ),
                                        base[:, :].unsqueeze(1).to_broadcast([P, TJ, NE]), ALU.add)\
                  .then_inc(placed, 1)
                dve.wait_ge(placed, b + 1)
                nc.vector.tensor_tensor(base[:, :], base[:, :], psT[:, TJ * NE:(TJ + 1) * NE], ALU.add)\
                  .then_inc(moved, 1)

            def s4f(b, q):
                dve.wait_ge(masked, b + 1)
                nc.vector.tensor_reduce(slf[:, :], tmp[:, :, :], AX.X, ALU.add)\
                  .then_inc(summed, 1)
                dve.wait_ge(summed, b + 1)
                need(dve, scattered[q], sent(q, b))
                nc.vector.tensor_copy(rows[:, q, :, D:D + K], idxf[:, :, :]).then_inc(noted, 1)
                nc.vector.tensor_copy(rows[:, q, :, D + K:ROW], places[:, bass.ds(b * TJ, TJ), :]).then_inc(noted, 1)
                nc.vector.tensor_copy(sli[:, q, :], slf[:, :]).then_inc(slotted, 1)

            def s4s(b, q):
                for s in range(NS):
                    dve.wait_ge(up_mm, b * NS + s + 1)
                    dve.wait_ge(r_gated, b * NS + s + 1)
                    need(dve, shared_mm, b)
                    nc.vector.tensor_tensor(hs[:, s, :], psQ[2 - 2 * s][:, :], sg[:, s, :], ALU.mult)\
                      .then_inc(hidden, 1)

            batch_pipeline(dve, {1: {"a": s1a, "n": s1n, "b": s1b, "m": s1m}, 2: {"a": s2a, "b": s2b},
                                 3: {"a": s3a, "b": s3b, "c": s3c, "n": s3n, "d": s3d},
                                 4: {"a": s4a, "n": s4n, "c": s4c, "g": s4g, "d": s4d, "f": s4f, "s": s4s}}, ORDER)
            plan_dve(dve)


def experts(nc, mem, sem, xs, ys):
    gu, down, ident, tile_e, tile_row = (mem[n] for n in ("gu", "down", "ident", "tile_e", "tile_row"))
    tile_eb, nowhere = mem["tile_eb"], mem["nowhere"]
    GR = 4
    NG = BLOCKS // GR
    with ExitStack() as ctx:
        def sb(name, shape, dt=F32):
            return ctx.enter_context(nc.sbuf_tensor(name, shape, dt))

        def ps(name):
            return ctx.enter_context(nc.psum_tensor(name, [P, 512], F32))

        NX = 2
        xb = sb("e_rows", [P, NX, GR, ROW])
        is_e, at_e = sb("e_is_expert", [P, GR, K]), sb("e_place_k", [P, GR, K])
        place, off = sb("e_place", [P, 2, GR]), sb("e_off", [P, 2, GR])
        dest = sb("e_dest", [P, 2, GR], I32)
        spare = sb("e_spare", [1, 1])
        xT = sb("e_rows_T", [P, 2, GR * P])
        sg = sb("e_silu", [P, 2, GR, F])
        hd = sb("e_hidden", [P, 2, GR, F])
        hTt = sb("e_hidden_T", [P, 2, GR * P])
        yb = sb("e_out", [P, 2, GR, D])
        psX, psH, psY = ps("ps_eX"), ps("ps_eH"), ps("ps_eY")
        psG = [ps(f"ps_eG{n}") for n in range(4)]
        block = ctx.enter_context(nc.Block())
        loaded = [sem(f"e_loaded{n}") for n in range(NX)]
        rows_T, rows_copied, gu_mm, silu, hidden = (sem("e_rows_T_ok"), sem("e_rows_copied"), sem("e_gu"),
                                                    sem("e_silu_ok"), sem("e_hidden_ok"))
        hid_T, hid_copied, down_mm, out_copied = (sem("e_hid_T"), sem("e_hid_copied"), sem("e_down"),
                                                  sem("e_out_copied"))
        stored = [sem(f"e_stored{n}") for n in range(2)]
        found, placed_k, placed, offed, dested, carried = (sem("e_found"), sem("e_placed_k"), sem("e_placed"),
                                                           sem("e_offed"), sem("e_dested"), sem("e_carried"))

        order = [(3, "a"), (2, "a"), (2, "b"), (3, "b"), (1, "a")]

        held = {}

        def pipeline(eng, **steps):
            def turn(g, q):
                if q == 0:
                    held.clear()
                for stage, step in order:
                    fn = steps.get(f"s{stage}{step}")
                    w = g - (stage - 1)
                    if fn is not None and (not isinstance(w, int) or 0 <= w < NG):
                        fn(w, (q + stage - 1) % 2)
            for g in range(4):
                turn(g, g % 2)
            with eng.Fori(2, NG // 2) as t:
                turn(t * 2, 0)
                turn(t * 2 + 1, 1)
            for g in range(NG, NG + 2):
                turn(g, g % 2)

        def read(engine, table, first, count, top):
            return nc.values_load_multi_w_load_instructions(table[0:1, bass.ds(first, count)], engines=(engine,),
                                                            min_val=0, max_val=top)[1]

        def experts_of(g, q):
            if q in held:
                return held[q]
            v = nc.tensor.value_load(tile_e[0:1, bass.ds(g, 1)], min_val=0, max_val=NE ** GR - 1)
            held[q] = [(v // NE ** n) % NE for n in range(GR)]
            return held[q]

        def turns_of(g, q, n):
            return (g // 2 + 1) * n if isinstance(g, int) else (g - q) * (n // 2) + n

        @block.sync
        def _(sp):
            def load(g, q):
                need(sp, rows_T, g - 1)
                need(sp, placed_k, g - 1)
                rows = read(mybir.EngineType.SP, tile_row, g * GR, GR, NE * REGION - P)
                for n in range(GR):
                    sp.dma_start(xb[:, q, n, :], xs[bass.ds(rows[n], P), :]).then_inc(loaded[q], 16)
            pipeline(sp, s1a=load)

        @block.gpsimd
        def _(pool):
            def store(g, q):
                pool.wait_ge(out_copied, g + 1)
                pool.wait_ge(dested, g + 1)
                need(pool, carried, g)
                nc.gpsimd.tensor_tensor(spare[:, :], ident[0:1, 0:1], ident[0:1, 0:1], ALU.add).then_inc(carried, 1)
                for n in range(GR):
                    pool.indirect_dma_start(
                        out=ys, out_offset=bass.IndirectOffsetOnAxis(ap=dest[:, q, n:n + 1], axis=0),
                        in_=yb[:, q, n, :], in_offset=None).then_inc(stored[q], 16)
            pipeline(pool, s3b=store)
            for q in range(2):
                pool.wait_ge(stored[q], 16 * GR * (NG // 2))

        @block.tensor
        def _(pe):
            def turn_rows(g, q):
                pe.wait_ge(loaded[q], turns_of(g, q, 16 * GR))
                need(pe, rows_copied, g)
                for n in range(GR):
                    mm = nc.tensor.transpose(psX[:, n * P:(n + 1) * P], xb[:, q, n, 0:D], ident[:, :])
                mm.then_inc(rows_T, 1)

            def gate_up(m):
                def step(g, q):
                    if m == 0:
                        held.pop(q, None)
                    es = experts_of(g, q)[2 * m:2 * m + 2]
                    if m == 0:
                        pe.wait_ge(rows_copied, g + 1)
                        need(pe, hidden, (g - 1) * 2)
                    for n in range(2):
                        mm = nc.tensor.matmul(psG[2 * q + m][:, n * 2 * F:(n + 1) * 2 * F],
                                              xT[:, q, (2 * m + n) * P:(2 * m + n + 1) * P],
                                              gu[:, bass.ds(es[n] * (2 * F), 2 * F)],
                                              start=True, stop=True)
                    mm.then_inc(gu_mm, 1)
                return step

            def turn_hidden(g, q):
                pe.wait_ge(hidden, g * 2 + 2)
                need(pe, hid_copied, g)
                for n in range(GR):
                    mm = nc.tensor.transpose(psH[:, n * P:(n + 1) * P], hd[:, q, n, :], ident[:, :])
                mm.then_inc(hid_T, 1)

            def out_rows(g, q):
                es = experts_of(g, q)
                pe.wait_ge(hid_copied, g + 1)
                need(pe, out_copied, g)
                for n in range(GR):
                    mm = nc.tensor.matmul(psY[:, n * P:(n + 1) * P], hTt[:, q, n * P:(n + 1) * P],
                                          down[:, bass.ds(es[n] * D, D)],
                                          start=True, stop=True)
                mm.then_inc(down_mm, 1)
            pipeline(pe, s1a=turn_rows, s2a=gate_up(0), s2b=gate_up(1), s3a=turn_hidden, s3b=out_rows)

        @block.scalar
        def _(act):
            def copy_rows(g, q):
                act.wait_ge(rows_T, g + 1)
                need(act, gu_mm, (g - 1) * 2)
                nc.scalar.activation(xT[:, q, :], psX[:, :], ACT.Copy).then_inc(rows_copied, 1)

            def gate(m):
                def step(g, q):
                    act.wait_ge(gu_mm, g * 2 + m + 1)
                    need(act, hidden, (g - 1) * 2)
                    nc.scalar.activation(sg[:, q, 2 * m:2 * m + 2, :],
                                         psG[2 * q + m][:, :].rearrange("p (n a f) -> p n a f", n=2, a=2)[:, :, 0, :],
                                         ACT.Silu).then_inc(silu, 1)
                return step

            def copy_out(g, q):
                act.wait_ge(down_mm, g + 1)
                if not isinstance(g, int) or g >= 2:
                    act.wait_ge(stored[q], turns_of(g, q, 16 * GR) - 16 * GR)
                nc.scalar.activation(yb[:, q].rearrange("p n d -> p (n d)"), psY[:, :], ACT.Copy)\
                  .then_inc(out_copied, 1)
            pipeline(act, s1a=copy_rows, s2a=gate(0), s2b=gate(1), s3b=copy_out)

        @block.vector
        def _(dve):
            def multiply(m):
                def step(g, q):
                    dve.wait_ge(silu, g * 2 + m + 1)
                    need(dve, hid_T, g - 1)
                    nc.vector.tensor_tensor(hd[:, q, 2 * m:2 * m + 2, :], sg[:, q, 2 * m:2 * m + 2, :],
                                            psG[2 * q + m][:, :].rearrange("p (n a f) -> p n a f", n=2, a=2)
                                            [:, :, 1, :], ALU.mult).then_inc(hidden, 1)
                return step

            def find_places(g, q):
                def tiles(table):
                    return table[:, bass.ds(g * GR, GR)]
                dve.wait_ge(loaded[q], turns_of(g, q, 16 * GR))
                need(dve, placed_k, g)
                nc.vector.tensor_tensor(is_e[:, :, :], xb[:, q, :, D:D + K],
                                        tiles(tile_eb).unsqueeze(2).to_broadcast([P, GR, K]), ALU.is_equal)\
                  .then_inc(found, 1)
                dve.wait_ge(found, g + 1)
                need(dve, placed, g)
                nc.vector.tensor_tensor(at_e[:, :, :], is_e[:, :, :], xb[:, q, :, D + K:ROW], ALU.mult)\
                  .then_inc(placed_k, 1)
                dve.wait_ge(placed_k, g + 1)
                need(dve, dested, g - 1)
                nc.vector.tensor_reduce(place[:, q, :], at_e[:, :, :], AX.X, ALU.add).then_inc(placed, 1)
                dve.wait_ge(placed, g + 1)
                nc.vector.scalar_tensor_tensor(out=off[:, q, :], in0=place[:, q, :], scalar=0.0, in1=tiles(nowhere),
                                               op0=ALU.is_equal, op1=ALU.mult).then_inc(offed, 1)

            def index_places(g, q):
                dve.wait_ge(offed, g + 1)
                if not isinstance(g, int) or g >= 2:
                    dve.wait_ge(stored[q], turns_of(g, q, 16 * GR) - 16 * GR)
                nc.vector.tensor_tensor(dest[:, q, :], place[:, q, :], off[:, q, :], ALU.add).then_inc(dested, 1)

            def copy_hidden(g, q):
                dve.wait_ge(hid_T, g + 1)
                need(dve, down_mm, g - 1)
                nc.vector.tensor_copy(hTt[:, q, :], psH[:, :]).then_inc(hid_copied, 1)
                index_places(g, q)
            pipeline(dve, s1a=find_places, s2a=multiply(0), s2b=multiply(1), s3a=copy_hidden)


def combine(nc, mem, sem, ys, out):
    res, wts, ident = mem["hT"], mem["wts"], mem["ident"]
    pairs = TILES // 2
    ys_v = ys[PLACE0:PLACE0 + N * K, :].rearrange("(n j p k) d -> n p j (k d)", j=2, p=P, k=K)
    out_v = out.rearrange("b t d -> (b t) d").rearrange("(n j p) d -> n p j d", j=2, p=P)
    with ExitStack() as ctx:
        NB = 4
        yg = ctx.enter_context(nc.sbuf_tensor("c_rows", [P, NB, 2, K, D], F32))
        acc = ctx.enter_context(nc.sbuf_tensor("c_acc", [P, NB, 2, D], F32))
        ps = [ctx.enter_context(nc.psum_tensor(f"ps_c{n}", [P, 512], F32)) for n in range(2)]
        block = ctx.enter_context(nc.Block())
        added, done, weighed, summed, copied = (sem("c_added"), sem("c_done"), sem("c_weighed"), sem("c_summed"),
                                                sem("c_copied"))
        fetched = [sem(f"c_fetched{n}") for n in range(NB)]
        stored = [sem(f"c_stored{n}") for n in range(NB)]

        def loop(eng, body):
            for t in range(2 * NB):
                body(t, t % NB)
            with eng.Fori(2, pairs // NB) as r:
                for n in range(NB):
                    body(r * NB + n, n)

        def earlier(t, n):
            return (t - n) * (16 // NB)

        def weight(t, j, k):
            return wts[:, bass.ds((t * 2 + j) * K + k, 1)]

        @block.sync
        def _(sp):
            def fetch(t, n):
                sp.dma_start(yg[:, n].rearrange("p j k d -> p j (k d)"),
                             ys_v[bass.ds(t, 1)].rearrange("o p j f -> (o p) j f")).then_inc(fetched[n], 16)

            def body(t, n):
                sp.wait_ge(done, t + 1)
                sp.wait_ge(copied, t + 1)
                dst = out_v[bass.ds(t, 1)].rearrange("o p j d -> (o p) j d")
                sp.dma_start(dst, acc[:, n]).then_inc(stored[n], 16)

            for n in range(NB):
                fetch(n, n)
            for t in range(NB):
                body(t, t)
                fetch(t + NB, t)
            with sp.Fori(1, pairs // NB - 1) as r:
                for n in range(NB):
                    body(r * NB + n, n)
                    fetch(r * NB + (n + NB), n)
            for n in range(NB):
                body(pairs - NB + n, n)
            for n in range(NB):
                sp.wait_ge(stored[n], 16 * (pairs // NB))

        @block.vector
        def _(dve):
            def body(t, n):
                dve.wait_ge(fetched[n], earlier(t, n) + 16)
                need(dve, stored[n], earlier(t, n))
                for k in range(K):
                    src = res[:, bass.ds(t * (2 * D), D)] if k == 0 else acc[:, n, 0, :]
                    if k:
                        dve.wait_ge(added, t * (K - 1) + k)
                    ins = nc.vector.scalar_tensor_tensor(out=acc[:, n, 0, :], in0=yg[:, n, 0, k, :],
                                                         scalar=weight(t, 0, k), in1=src,
                                                         op0=ALU.mult, op1=ALU.add)
                    ins.then_inc(added if k < K - 1 else done, 1)
            loop(dve, body)

        @block.scalar
        def _(act):
            def copy(t, n):
                act.wait_ge(summed, t + 1)
                need(act, stored[n], earlier(t, n))
                nc.scalar.activation(acc[:, n, 1, :], ps[n % 2][:, 0:D], ACT.Copy).then_inc(copied, 1)

            def body(t, n):
                act.wait_ge(fetched[n], earlier(t, n) + 16)
                for k in range(K):
                    nc.scalar.activation(yg[:, n, 1, k, :], yg[:, n, 1, k, :], ACT.Copy, scale=weight(t, 1, k))\
                      .then_inc(weighed, 1)
                if not isinstance(t, int) or t > 0:
                    copy(t - 1, (n - 1) % NB)
            loop(act, body)
            copy(pairs - 1, NB - 1)

        @block.tensor
        def _(pe):
            def body(t, n):
                pe.wait_ge(weighed, t * K + K)
                need(pe, copied, t - 1)
                nc.tensor.matmul(ps[n % 2][:, 0:D], ident[:, :], res[:, bass.ds(t * (2 * D) + D, D)],
                                 start=True, stop=False)
                for k in range(K):
                    mm = nc.tensor.matmul(ps[n % 2][:, 0:D], ident[:, :], yg[:, n, 1, k, :],
                                          start=False, stop=(k == K - 1))
                mm.then_inc(summed, 1)
            loop(pe, body)


def build(nc, x, tok_wT, par_d, proj_w, out_w, cosT, sinT, wr, shared_gu, shared_d, gu, down, out):
    with ExitStack() as ctx:
        def sb(name, shape, dt=F32):
            return ctx.enter_context(nc.sbuf_tensor(name, shape, dt))

        def sem(name):
            return ctx.enter_context(nc.semaphore(name))

        mem = {
            "hT": sb("hT", [P, N]),
            "ident": sb("ident", [P, P]),
            "par": sb("par", [P, NPAR]),
            "tok_wT": sb("tok_wT_sb", [P, P]),
            "w": sb("proj_w_sb", [P, 5 * P]),
            "ow": sb("out_w_sb", [P, 2, P]),
            "cos": sb("cos_sb", [P, T]),
            "sin": sb("sin_sb", [P, T]),
            "wr": sb("wr_sb", [P, NE]),
            "shared_gu": sb("shared_gu_sb", [P, NS, 2, F]),
            "shared_d": sb("shared_d_sb", [P, NS, D]),
        }
        w_loaded = sem("w_loaded")
        with nc.Block() as block:
            consts, zeroed = sem("consts_loaded"), sem("ident_zeroed")
            made = sem("ident_made")

            @block.sync
            def _(sp):
                sp.dma_start(mem["tok_wT"][:, :], tok_wT).then_inc(consts, 16)
                sp.dma_start(mem["par"][:, :], par_d).then_inc(consts, 16)
                sp.wait_ge(consts, 32)

            @block.gpsimd
            def _(pool):
                nc.gpsimd.memset(mem["ident"][:, :], 0.0).then_inc(zeroed, 1)
                pool.wait_ge(zeroed, 1)
                nc.gpsimd.affine_select(out=mem["ident"][:, :], in_=mem["ident"][:, :], compare_op=ALU.not_equal,
                                        fill=1.0, base=0, pattern=[[-1, P]], channel_multiplier=1).then_inc(made, 1)
                pool.wait_ge(made, 1)
        later = ((mem["w"], proj_w), (mem["ow"], out_w), (mem["cos"], cosT), (mem["sin"], sinT),
                 (mem["wr"], wr), (mem["shared_gu"], shared_gu), (mem["shared_d"], shared_d))
        pool_chunks(nc, mem, sem, x, later, w_loaded)
        xs = nc.dram_tensor("xs", (NE * REGION, ROW), F32, kind="Internal").ap()
        ys = nc.dram_tensor("ys", (PLACE0 + N * K, D), F32, kind="Internal").ap()
        arena = sb("arena", [P, NE * 3 * F])
        mem |= {
            "arena": arena,
            "gu": arena[:, 0:NE * 2 * F],
            "down": arena[:, NE * 2 * F:],
            "wts": sb("wts", [P, TILES * K]),
            "tile_eb": sb("tile_eb", [P, BLOCKS]),
            "nowhere": sb("nowhere", [P, BLOCKS]),
            "iota": sb("iota", [P, NE]),
            "base": sb("next_row", [P, NE]),
            "tile_e": sb("tile_e", [1, BLOCKS // 4], I32),
            "tile_row": sb("tile_row", [1, BLOCKS], I32),
        }
        attend_and_route(nc, mem, sem, w_loaded, gu, down, xs)
        experts(nc, mem, sem, xs, ys)
        combine(nc, mem, sem, ys, out)


def kernel(**inputs):
    import numpy as _np
    import concourse.bacc as _bacc
    from concourse import mybir as _mybir
    from concourse.bass_utils import run_bass_kernel_spmd as _run

    a = {k: _np.asarray(v) for k, v in inputs.items()}
    L = "L0_attn_"

    def halves(v):
        return v.reshape(2, P).T

    swap = _np.arange(P) ^ 1
    cw = {n: a[L + n + "_cw"] for n in ("u", "v", "qk")}
    cols = [a["L0_tok_b"][:, None]]
    cols += [a[L + n + "_ln_g"][:, None] for n in ("u", "v", "qk")]
    cols += [a[L + n + "_ln_b"][:, None] for n in ("u", "v", "qk")]
    cols += [halves(a[L + "u_b"]), halves(a[L + "v_b"]), a[L + "qk_b"][:, None]]
    for t in range(3):
        cols += [halves(cw["u"][:, t]), halves(cw["v"][:, t]), cw["qk"][:, t:t + 1]]
    cols += [halves(a[L + "u_cb"]), halves(a[L + "v_cb"]), a[L + "qk_cb"][:, None]]
    cols += [halves(a[L + "out_ln_g"]), halves(a[L + "out_ln_b"]), a[L + "out_b"][:, None]]
    cols += [a[L + "out_cw"], a[L + "out_cb"][:, None]]
    cols += [a[L + "gamma"].T, a[L + "beta"].T, a[L + "gamma"].T[swap], a[L + "beta"].T[swap]]
    inv = (1.0 / 10000.0 ** (_np.arange(0, D, 2, dtype=_np.float32) / _np.float32(D))).astype(_np.float32)
    ang = _np.repeat(_np.arange(T, dtype=_np.float32)[:, None] * inv, 2, axis=-1)
    sign = _np.where(_np.arange(D) % 2 == 0, -1.0, 1.0).astype(_np.float32)[:, None]
    laid = {
        "x": a["x"],
        "tok_wT": a["L0_tok_W"].T,
        "par": _np.concatenate(cols, axis=1),
        "proj_w": _np.concatenate([a[L + "u_w"], a[L + "v_w"], a[L + "qk_w"]], axis=1),
        "out_w": a[L + "out_w"].reshape(2, P, P).transpose(1, 0, 2),
        "cosT": _np.cos(ang).T.astype(_np.float32),
        "sinT": _np.sin(ang).T.astype(_np.float32) * sign,
        "wr": a["L0_ffn_Wr"],
        "shared_gu": _np.stack([a["L0_ffn_sWg"], a["L0_ffn_sWu"]], axis=2).transpose(1, 0, 2, 3),
        "shared_d": a["L0_ffn_sWd"].transpose(1, 0, 2),
        "gu": _np.stack([a["L0_ffn_Wg"], a["L0_ffn_Wu"]], axis=2).transpose(1, 0, 2, 3),
        "down": a["L0_ffn_Wd"].transpose(1, 0, 2),
    }
    nc = _bacc.Bacc("TRN2", target_bir_lowering=False, num_devices=1)
    arrays, args = {}, []
    for name, v in laid.items():
        v = _np.ascontiguousarray(v)
        arrays[f"in_{name}"] = v
        args.append(nc.dram_tensor(f"in_{name}", v.shape, _mybir.dt.from_np(v.dtype), kind="ExternalInput").ap())
    args.append(nc.dram_tensor("out_h", (B, T, D), F32, kind="ExternalOutput").ap())
    build(nc, *args)
    r = _run(nc, [arrays], core_ids=[0])
    return r.results[0]["out_h"]
```
